# Optimizing a Trainium2 kernel written in Bass

```python
import numpy as np
import jax
import jax.numpy as jnp

def _softmax(x, axis=-1):
    return jax.nn.softmax(x, axis=axis)

def _gelu(x):
    return jax.nn.gelu(x, approximate=True)

def _silu(x):
    return jax.nn.silu(x)

def _sigmoid(x):
    return jax.nn.sigmoid(x)

def _layernorm(x, axis=-1, eps=1e-05):
    m = jnp.mean(x, axis=axis, keepdims=True)
    v = jnp.var(x, axis=axis, keepdims=True)
    return (x - m) / jnp.sqrt(v + eps)

def _scatter_add(tgt, idx, src, axis=0):
    return tgt.at[idx].add(src)

def _segment_sum(src, seg, n):
    return jax.ops.segment_sum(src, seg, n)
kernel_name = 'mk_gnn_resnorm_d1_gnn_r8_304728'

def setup_inputs(seed: int=0):
    np.random.seed(seed)
    _w = jnp.asarray

    def _rec_inputs():
        import jax
        import jax.numpy as jnp
        _gk = jax.random.key(seed)
        x = -0.000202 + 1 * jax.random.normal(jax.random.fold_in(_gk, 1), (12500, 64), jnp.float32)
        src = jax.random.randint(jax.random.fold_in(_gk, 2), (400000,), 0, 12500, jnp.int32)
        dst = jax.random.randint(jax.random.fold_in(_gk, 3), (400000,), 0, 12500, jnp.int32)
        _o = jnp.argsort(dst, stable=True)
        src = src[_o]
        dst = dst[_o]
        edge_attr_16 = 0.000196303 + 1.00016 * jax.random.normal(jax.random.fold_in(_gk, 11), (400000, 16), jnp.float32)
        return (x, src, dst, edge_attr_16)
    x, src, dst, edge_attr_16 = _rec_inputs()

    def _L0_gnn_setup():
        import jax, jax.numpy as jnp
        import numpy as np
        N_NODES = 12500
        N_EDGES = 200000
        HIDDEN = 64
        EDGE_DIM = 16
        key = jax.random.key(seed)
        ks = jax.random.split(key, 9)
        x = jax.random.normal(ks[0], (N_NODES, HIDDEN), dtype=jnp.float32)
        edge_index = jax.random.randint(ks[1], (2, N_EDGES), 0, N_NODES, dtype=jnp.int32)
        edge_attr = jax.random.normal(ks[2], (N_EDGES, EDGE_DIM), dtype=jnp.float32)
        s1 = 1.0 / np.sqrt(HIDDEN * 2 + EDGE_DIM)
        s2 = 1.0 / np.sqrt(HIDDEN)
        s3 = 1.0 / np.sqrt(HIDDEN * 2)
        W1 = jax.random.uniform(ks[3], (HIDDEN * 2 + EDGE_DIM, HIDDEN), jnp.float32, -s1, s1)
        b1 = jax.random.uniform(ks[4], (HIDDEN,), jnp.float32, -s1, s1)
        W2 = jax.random.uniform(ks[5], (HIDDEN, HIDDEN), jnp.float32, -s2, s2)
        b2 = jax.random.uniform(ks[6], (HIDDEN,), jnp.float32, -s2, s2)
        W3 = jax.random.uniform(ks[7], (HIDDEN * 2, HIDDEN), jnp.float32, -s3, s3)
        b3 = jax.random.uniform(ks[8], (HIDDEN,), jnp.float32, -s3, s3)
        return {'x': x, 'edge_index': edge_index, 'edge_attr': edge_attr, 'W1': W1, 'b1': b1, 'W2': W2, 'b2': b2, 'W3': W3, 'b3': b3}
    _L0_gnn_all = _L0_gnn_setup()
    _L0_gnn_in = {k: v for k, v in _L0_gnn_all.items() if k in ('W1', 'b1', 'W2', 'b2', 'W3', 'b3')}
    del _L0_gnn_all
    return {'x': x, 'src': src, 'dst': dst, 'edge_attr_16': edge_attr_16, 'L0_gnn_W1': _L0_gnn_in['W1'], 'L0_gnn_b1': _L0_gnn_in['b1'], 'L0_gnn_W2': _L0_gnn_in['W2'], 'L0_gnn_b2': _L0_gnn_in['b2'], 'L0_gnn_W3': _L0_gnn_in['W3'], 'L0_gnn_b3': _L0_gnn_in['b3']}

def reference(x, src, dst, edge_attr_16, L0_gnn_W1, L0_gnn_b1, L0_gnn_W2, L0_gnn_b2, L0_gnn_W3, L0_gnn_b3):
    import jax
    import jax.numpy as jnp

    def _L0_gnn_ref(x, edge_index, edge_attr, W1, b1, W2, b2, W3, b3):
        import jax, jax.numpy as jnp
        import numpy as np
        N_NODES = 12500
        N_EDGES = 200000
        HIDDEN = 64
        EDGE_DIM = 16
        src, dst = (edge_index[0], edge_index[1])
        m_in = jnp.concatenate([x[src], x[dst], edge_attr], axis=-1)
        h = jax.nn.silu(m_in @ W1 + b1)
        messages = jax.nn.silu(h @ W2 + b2)
        agg = jax.ops.segment_sum(messages, dst, num_segments=x.shape[0])
        node_in = jnp.concatenate([x, agg], axis=-1)
        return jax.nn.silu(node_in @ W3 + b3)
    edge_index = jnp.stack([src, dst])
    x = _layernorm(x + _L0_gnn_ref(x, edge_index, edge_attr_16, L0_gnn_W1, L0_gnn_b1, L0_gnn_W2, L0_gnn_b2, L0_gnn_W3, L0_gnn_b3), axis=-1)
    return x

_drawn_inputs = setup_inputs


def setup_inputs(seed=0):
    import zlib

    import numpy as np

    out = dict(_drawn_inputs(seed))
    spreads = {}
    factors = {}
    for name, (base, spread) in spreads.items():
        noise = np.random.default_rng([zlib.crc32(name.encode()), seed]).standard_normal(out[name].shape)
        drawn = base * np.exp(spread * noise) if base else spread * noise
        out[name] = jnp.asarray(drawn.astype(out[name].dtype))
    for name, factor in factors.items():
        out[name] = (out[name] * factor).astype(out[name].dtype)
    return out
```

```python
import concourse.bass as bass
import concourse.mybir as mybir
from contextlib import ExitStack


def gnn_layer(nc, x, src, dst, edge_attr, W1, b1, W2, b2, W3, b3, out):
    F32, I32 = mybir.dt.float32, mybir.dt.int32
    ALU, ACT, AX = mybir.AluOpType, mybir.ActivationFunctionType, mybir.AxisListType

    P = 128
    N, H = x.shape
    E, D = edge_attr.shape
    T = 8
    G = P * T
    FULL = E // G
    TT = (E - FULL * G) // P
    assert 0 < TT < T and E == FULL * G + TT * P and 2 * H == P and T * D == P
    NG = FULL + 1
    WIN = 64
    LASTW = N - WIN
    NT = -(-N // P)
    NPAD = NT * P
    NREM = N - (NT - 1) * P
    S = 3
    assert FULL % S == 0
    QF = FULL // P
    QR = FULL - QF * P
    Q = QF + 1
    EPS = 1e-5
    C = T * H
    NB = 4
    OB = 8
    NOB = -(-NT // OB)

    ctx = ExitStack()
    with ctx:
        def sb(name, shape, dt=F32):
            return ctx.enter_context(nc.sbuf_tensor(name, shape, dt))

        def pb(name, shape):
            return ctx.enter_context(nc.psum_tensor(name, shape, F32))

        def sem(name):
            return ctx.enter_context(nc.semaphore(name))

        node_T = sb("node_T", [P, NPAD])
        xs = sb("xs", [P, NT, H])
        ident = sb("ident", [P, P])
        iota = sb("iota", [P, P])
        ones = sb("ones", [P, P])
        w1a_bd = sb("w1a_bd", [P, P])
        w1b_bd = sb("w1b_bd", [P, P])
        w2_bd = sb("w2_bd", [P, P])
        w1c_bd = sb("w1c_bd", [P, C])
        w3 = sb("w3", [P, H])
        b1_bc = sb("b1_bc", [P, H])
        b1_rep = sb("b1_rep", [1, C])
        b2_rep = sb("b2_rep", [1, C])
        b3_rep = sb("b3_rep", [1, C])
        base_bc = sb("base_bc", [P, Q * P])
        base_i = sb("base_i", [1, Q * P], I32)
        no_node = sb("no_node", [P, T], I32)
        dst_g = sb("dst_g", [P, Q, G], I32)
        hi = sb("hi", [P, Q])
        lo = sb("lo", [P, Q])
        base_g = sb("base_g", [P, Q])
        base_diag = sb("base_diag", [P, Q, P])
        outside = sb("outside", [P, 1])
        outside_all = sb("outside_all", [1, 1])
        general_i = sb("general_i", [1, 1], I32)
        src_i = sb("src_i", [P, S, T], I32)
        dst_i = sb("dst_i", [P, S, T], I32)
        ea = sb("ea", [P, S, P])
        xg = sb("xg", [P, S, T, H])
        onehot = sb("onehot", [P, S, T, WIN])
        msg = sb("msg", [P, S, C])
        dst_rel = sb("dst_rel", [P, T])
        xwin = sb("xwin", [H, 2, WIN])
        xg_T = sb("xg_T", [P, C])
        oh_T = sb("oh_T", [P, C])
        ea_T = sb("ea_T", [P, P])
        bwin_bd = sb("bwin_bd", [P, P])
        h = sb("h", [P, C])
        h_T = sb("h_T", [P, C])
        upd = sb("upd", [P, 2, C])
        square = sb("square", [P, 2, C])
        mean = sb("mean", [P, NT])
        var = sb("var", [P, NT])
        rstd = sb("rstd", [P, NT])
        done_mark = sb("done_mark", [1, 1])

        xg_ps = pb("xg_ps", [P, C])
        oh_ps = pb("oh_ps", [P, C])
        z1_ps = pb("z1_ps", [P, C])
        h_ps = pb("h_ps", [P, C])
        z2_ps = pb("z2_ps", [P, C])
        ea_ps = pb("ea_ps", [P, C])
        agg_ps = pb("agg_ps", [P, C])
        bwin_ps = pb("bwin_ps", [P, C])

        s_zeroed = sem("zeroed")
        s_ident = sem("ident_made")
        s_const = sem("constants_made")
        s_dst_g = sem("dst_g_loaded")
        s_x = sem("x_loaded")
        s_w = sem("weights_loaded")
        s_chk = sem("check_step")
        s_base = sem("base_spread")
        s_out_T = sem("outside_transposed")
        s_flag = sem("general_known")
        s_xT_ps = sem("x_transposed")
        s_xT_a = sem("x_T_copied_act")
        s_xT_v = sem("x_T_copied_dve")
        s_src = [sem(f"src_loaded{s}") for s in range(S)]
        s_dst = [sem(f"dst_loaded{s}") for s in range(S)]
        s_ea = [sem(f"ea_loaded{s}") for s in range(S)]
        s_xg = [sem(f"x_gathered{s}") for s in range(S)]
        s_xwin = sem("window_copied")
        s_rel = sem("dst_rel_made")
        s_oh = sem("onehot_made")
        s_in_T = sem("inputs_transposed")
        s_bwin = sem("window_projected")
        s_oh_T = sem("onehot_transposed")
        s_xgc = sem("xg_T_copied")
        s_eac = sem("ea_T_copied")
        s_bwc = sem("window_biased")
        s_ohc = sem("oh_T_copied")
        s_z1 = sem("z1_done")
        s_h = sem("h_done")
        s_hT = sem("h_transposed")
        s_hTc = sem("h_T_copied")
        s_z2 = sem("z2_done")
        s_msg = sem("messages_done")
        s_agg = sem("window_summed")
        s_added = sem("window_added")
        a_load = sem("any_loaded")
        a_xs = sem("any_x_src_gathered")
        a_xd = sem("any_x_dst_gathered")
        a_rel = sem("any_dst_rel_made")
        a_T = sem("any_inputs_transposed")
        a_Tc = sem("any_inputs_copied")
        a_z1 = sem("any_z1_done")
        a_h = sem("any_h_done")
        a_hT = sem("any_h_transposed")
        a_hTc = sem("any_h_T_copied")
        a_z2 = sem("any_z2_done")
        a_msg = sem("any_messages_done")
        a_oh = sem("any_onehot_made")
        a_agg = sem("any_window_summed")
        a_added = sem("any_window_added")
        s_sums = sem("sums_complete")
        s_z3 = sem("z3_done")
        s_upd = sem("update_done")
        s_res = sem("residual_added")
        s_cen = sem("centred")
        s_sq = sem("squared")
        s_sqr = sem("squares_summed")
        s_var = sem("variance_done")
        s_std = sem("std_done")
        s_rstd = sem("rstd_done")
        s_norm = sem("normalised")
        s_out = sem("out_stored")

        SRC, DST = 0, 1
        onehot_any = onehot[:, 0:2, :, :].rearrange("p s t n -> p (s t n)").rearrange("p (t n) -> p t n", n=P)

        block = ctx.enter_context(nc.Block())

        src_v = src[0:FULL * G].rearrange("(g p t) -> g p t", p=P, t=T)
        dst_v = dst[0:FULL * G].rearrange("(g p t) -> g p t", p=P, t=T)
        ea_v = edge_attr[0:FULL * G, :].rearrange("(g p t) d -> g p (t d)", p=P, t=T)
        src_tail = src[FULL * G:E].rearrange("(p t) -> p t", t=TT)
        dst_tail = dst[FULL * G:E].rearrange("(p t) -> p t", t=TT)
        ea_tail = edge_attr[FULL * G:E, :].rearrange("(p t) d -> p (t d)", t=TT)
        N0 = (NT - 1) * P
        N_X = 2
        n_weights = 6 + T + 5
        store_cuts = [0, 26, 52, 78, NT - 1]
        xT_banks = [(k, min(k + NB, NT)) for k in range(0, NT, NB)]

        def rows(w):
            return w.rearrange("(a n) -> a n", a=1)

        @block.sync
        def _(sp):
            def load_group(n, g, s):
                sp.dma_start(src_i[:, s, :], src_v[g]).then_inc(s_src[s], 16)
                sp.dma_start(dst_i[:, s, :], dst_v[g]).then_inc(s_dst[s], 16)
                sp.dma_start(ea[:, s, :], ea_v[g]).then_inc(s_ea[s], 16)

            def load_tail(s):
                sp.dma_start(src_i[:, s, 0:TT], src_tail).then_inc(s_src[s], 16)
                sp.dma_start(dst_i[:, s, 0:TT], dst_tail).then_inc(s_dst[s], 16)
                sp.dma_start(dst_i[:, s, TT:T], no_node[:, TT:T]).then_inc(s_dst[s], 16)
                sp.dma_start(ea[:, s, 0:TT * D], ea_tail).then_inc(s_ea[s], 16)

            sp.wait_ge(s_zeroed, 1)
            sp.dma_start(dst_g[:, 0:QF, :],
                         dst[0:QF * P * G].rearrange("(q p e) -> p q e", p=P, e=G)).then_inc(s_dst_g, 16)
            sp.dma_start(dst_g[0:QR, QF, :],
                         dst[QF * P * G:FULL * G].rearrange("(p e) -> p e", e=G)).then_inc(s_dst_g, 16)
            sp.dma_start(dst_g[QR:QR + 1, QF, 0:TT * P], rows(dst[FULL * G:E])).then_inc(s_dst_g, 16)
            sp.dma_start(dst_g[QR:QR + 1, QF, TT * P:G],
                         rows(dst[FULL * G:FULL * G + G - TT * P])).then_inc(s_dst_g, 16)
            sp.dma_start(xs[:, 0:NT - 1, :],
                         x[0:N0, :].rearrange("(k p) f -> p k f", p=P)).then_inc(s_x, 16)
            sp.dma_start(xs[0:NREM, NT - 1, :], x[N0:N, :]).then_inc(s_x, 16)
            sp.wait_ge(s_flag, 1)
            general = sp.value_load(general_i[0:1, 0:1], min_val=0, max_val=1)
            with sp.If(general == 0):
                for g in range(S):
                    load_group(0, g, g)
                with sp.Fori(1, FULL // S) as k:
                    for s in range(S):
                        sp.wait_ge(s_rel, k * S + (s - S + 1))
                        sp.wait_ge(s_in_T, k * S + (s - S + 1))
                        sp.nop(nofuse=True)
                        load_group(k, k * S + s, s)
                sp.wait_ge(s_rel, FULL - S + 1)
                sp.wait_ge(s_in_T, FULL - S + 1)
                load_tail(0)
            with sp.Else():
                with sp.Fori(0, FULL) as g:
                    sp.wait_ge(a_added, g * NT)
                    sp.nop(nofuse=True)
                    sp.dma_start(src_i[:, 0, :], src_v[g]).then_inc(a_load, 16)
                    sp.dma_start(dst_i[:, 0, :], dst_v[g]).then_inc(a_load, 16)
                    sp.dma_start(ea[:, 0, :], ea_v[g]).then_inc(a_load, 16)
                sp.wait_ge(a_added, FULL * NT)
                sp.dma_start(src_i[:, 0, 0:TT], src_tail).then_inc(a_load, 16)
                sp.dma_start(dst_i[:, 0, 0:TT], dst_tail).then_inc(a_load, 16)
                sp.dma_start(ea[:, 0, 0:TT * D], ea_tail).then_inc(a_load, 16)
            for n in range(4):
                a, b = store_cuts[n], store_cuts[n + 1]
                sp.wait_ge(s_norm, n + 1)
                sp.dma_start(out[a * P:b * P, :].rearrange("(k p) f -> p k f", p=P),
                             xs[:, a:b, :]).then_inc(s_out, 16)
            sp.wait_ge(s_norm, 5)
            sp.dma_start(out[N0:N, :], xs[0:NREM, NT - 1, :]).then_inc(s_out, 16)
            sp.wait_ge(s_out, 5 * 16)

        @block.gpsimd
        def _(pool):
            nc.gpsimd.memset(ident[:], 0.0).then_inc(s_ident, 1)
            pool.wait_ge(s_ident, 1)
            nc.gpsimd.affine_select(out=ident[:], in_=ident[:], compare_op=ALU.not_equal, fill=1.0, base=0,
                                    pattern=[[-1, P]], channel_multiplier=1).then_inc(s_ident, 1)
            nc.gpsimd.iota(iota[:], pattern=[[1, P]], base=0, channel_multiplier=0,
                           allow_small_or_imprecise_dtypes=True).then_inc(s_const, 1)
            pool.wait_ge(s_const, 1)
            nc.gpsimd.memset(node_T[H:P, :], 0.0).then_inc(s_const, 1)
            pool.wait_ge(s_const, 2)
            nc.gpsimd.memset(no_node[:], -1).then_inc(s_const, 1)

            def gather(columns, s):
                for t in range(columns):
                    pool.indirect_dma_start(
                        out=xg[:, s, t, :], out_offset=None, in_=x[:, :],
                        in_offset=bass.IndirectOffsetOnAxis(ap=src_i[:, s, t:t + 1], axis=0),
                    ).then_inc(s_xg[s], 16)

            pool.wait_ge(s_flag, 1)
            general = pool.value_load(general_i[0:1, 0:1], min_val=0, max_val=1)
            with pool.If(general == 0):
                for s in range(S):
                    pool.wait_ge(s_src[s], 16)
                    gather(T, s)
                with pool.Fori(1, FULL // S) as k:
                    for s in range(S):
                        pool.wait_ge(s_in_T, k * S + (s - S + 1))
                        pool.wait_ge(s_src[s], k * 16 + 16)
                        pool.nop(nofuse=True)
                        gather(T, s)
                pool.wait_ge(s_in_T, FULL - S + 1)
                pool.wait_ge(s_src[0], 16 * (FULL // S + 1))
                gather(TT, 0)
            with pool.Else():
                def gather_both(columns):
                    for rows_of, i, arrived in ((SRC, src_i, a_xs), (DST, dst_i, a_xd)):
                        for t in range(columns):
                            pool.indirect_dma_start(
                                out=xg[:, rows_of, t, :], out_offset=None, in_=x[:, :],
                                in_offset=bass.IndirectOffsetOnAxis(ap=i[:, 0, t:t + 1], axis=0),
                            ).then_inc(arrived, 16)

                with pool.Fori(0, FULL) as g:
                    pool.wait_ge(a_load, g * 48 + 48)
                    pool.nop(nofuse=True)
                    gather_both(T)
                pool.wait_ge(a_load, FULL * 48 + 48)
                gather_both(TT)

        @block.scalar
        def _(act):
            act.wait_ge(s_zeroed, 1)
            loads = []
            for w, m in ((w1a_bd, W1[0:H, :]), (w1b_bd, W1[H:2 * H, :]), (w2_bd, W2)):
                loads += [(w[0:H, 0:H], m), (w[H:P, H:P], m)]
            for t in range(T):
                loads.append((w1c_bd[t * D:(t + 1) * D, t * H:(t + 1) * H], W1[2 * H:2 * H + D, :]))
            loads.append((w3[:, :], W3))
            loads.append((b1_bc[:, :], rows(b1).to_broadcast([P, H])))
            for rep, b in ((b1_rep, b1), (b2_rep, b2), (b3_rep, b3)):
                loads.append((rep[:, :].rearrange("a (t f) -> a t f", f=H),
                              b.rearrange("(a t f) -> a t f", a=1, t=1).to_broadcast([1, T, H])))
            assert len(loads) == n_weights
            for to, of in loads:
                act.dma_start(to, of).then_inc(s_w, 16)

            for n in range(0, len(xT_banks), 2):
                a, b = xT_banks[n]
                act.wait_ge(s_xT_ps, n + 1)
                nc.scalar.copy(node_T[0:H, a * P:b * P], xg_ps[0:H, 0:(b - a) * P]).then_inc(s_xT_a, 1)

            def first_silu(g):
                act.wait_ge(s_z1, g + 1)
                nc.scalar.activation(h[:, :], z1_ps[:, :], ACT.Silu).then_inc(s_h, 1)

            def copy_h_T(g):
                act.wait_ge(s_hT, g + 1)
                nc.scalar.copy(h_T[:, :], h_ps[:, :]).then_inc(s_hTc, 1)

            def second_silu(g, s):
                act.wait_ge(s_z2, g + 1)
                nc.scalar.activation(msg[:, s, :], z2_ps[:, :], ACT.Silu).then_inc(s_msg, 1)

            def square_tiles(n):
                a, b = n * OB, min(NT, n * OB + OB)
                act.wait_ge(s_cen, n + 1)
                if n >= 2:
                    act.wait_ge(s_sqr, n - 1)
                nc.scalar.activation(square[:, n % 2, 0:(b - a) * H],
                                     xs[:, a:b, :].rearrange("p k f -> p (k f)"), ACT.Square).then_inc(s_sq, 1)

            act.wait_ge(s_flag, 1)
            general = act.value_load(general_i[0:1, 0:1], min_val=0, max_val=1)
            with act.If(general == 0):
                first_silu(0)
                copy_h_T(0)
                with act.Fori(0, FULL // S) as k:
                    for u in range(S):
                        g = k * S + (u + 1)
                        second_silu(k * S + u, u)
                        first_silu(g)
                        copy_h_T(g)
                second_silu(FULL, FULL % S)
            with act.Else():
                with act.Fori(0, NG) as g:
                    act.wait_ge(a_z1, g + 1)
                    nc.scalar.activation(h[:, :], z1_ps[:, :], ACT.Silu).then_inc(a_h, 1)
                    act.wait_ge(a_hT, g + 1)
                    nc.scalar.copy(h_T[:, :], h_ps[:, :]).then_inc(a_hTc, 1)
                    act.wait_ge(a_z2, g + 1)
                    nc.scalar.activation(msg[:, 0, :], z2_ps[:, :], ACT.Silu).then_inc(a_msg, 1)

            for n in range(NOB):
                z = (z1_ps, z2_ps)[n % 2]
                m = min(OB, NT - n * OB) * H
                act.wait_ge(s_z3, n + 1)
                if n >= 2:
                    act.wait_ge(s_res, n - 1)
                nc.scalar.activation(upd[:, n % 2, 0:m], z[:, 0:m], ACT.Silu).then_inc(s_upd, 1)
                if n >= 1:
                    square_tiles(n - 1)
            square_tiles(NOB - 1)
            act.wait_ge(s_var, 1)
            nc.scalar.activation(rstd[:, :], var[:, :], ACT.Sqrt).then_inc(s_std, 1)

        @block.vector
        def _(dve):
            steps = [0]

            def step(ins):
                ins.then_inc(s_chk, 1)
                steps[0] += 1
                dve.wait_ge(s_chk, steps[0])

            nc.vector.memset(dst_g[:, QF, :], 0)
            for w in (w1a_bd, w1b_bd, w2_bd, w1c_bd, bwin_bd):
                nc.vector.memset(w[:, :], 0.0)
            nc.vector.memset(ones[:, :], 1.0)
            nc.vector.memset(xs[:, NT - 1, :], 0.0).then_inc(s_zeroed, 1)

            dve.wait_ge(s_dst_g, 4 * 16)
            nc.vector.tensor_reduce(hi[:, :], dst_g[:, :, :], AX.X, ALU.max)
            nc.vector.tensor_reduce(lo[:, :], dst_g[:, :, :], AX.X, ALU.min)
            step(nc.vector.tensor_scalar(base_g[:, :], dst_g[:, :, 0], float(LASTW), None, ALU.min))
            dve.wait_ge(s_ident, 2)
            for q in range(Q):
                last = nc.vector.tensor_scalar(base_diag[:, q, :], ident[:, :], base_g[:, q:q + 1], None, ALU.mult)
            step(last)
            nc.vector.tensor_sub(hi[:, :], hi[:, :], base_g[:, :])
            step(nc.vector.tensor_sub(lo[:, :], base_g[:, :], lo[:, :]))
            step(nc.vector.scalar_tensor_tensor(out=hi[:, :], in0=hi[:, :], scalar=float(1 - WIN), in1=lo[:, :],
                                                op0=ALU.add, op1=ALU.max))
            step(nc.vector.tensor_reduce(outside[:, :], hi[:, :], AX.X, ALU.max))
            dve.wait_ge(s_out_T, 1)
            step(nc.vector.tensor_reduce(outside_all[:, :], oh_ps[0:1, 0:P], AX.X, ALU.max))
            nc.vector.tensor_scalar(general_i[:, :], outside_all[:, :], 0.0, None, ALU.is_gt).then_inc(s_flag, 1)
            dve.wait_ge(s_base, 1)
            nc.vector.tensor_copy(base_bc[:, :], z1_ps[:, 0:Q * P])
            step(nc.vector.tensor_copy(base_i[:, :], z1_ps[0:1, 0:Q * P]))

            for n in range(1, len(xT_banks), 2):
                a, b = xT_banks[n]
                dve.wait_ge(s_xT_ps, n + 1)
                nc.vector.tensor_copy(node_T[0:H, a * P:b * P], oh_ps[0:H, 0:(b - a) * P]).then_inc(s_xT_v, 1)

            def window_start(g):
                return dve.value_load(base_i[0:1, bass.ds(g, 1)], min_val=0, max_val=LASTW)

            def prepare(g, s, arrived):
                at = window_start(g)
                nc.vector.tensor_scalar(xwin[:, :, :],
                                        node_T[0:H, bass.ds(at, WIN)].unsqueeze(1).to_broadcast([H, 2, WIN]),
                                        1.0, None, ALU.mult).then_inc(s_xwin, 1)
                dve.wait_ge(s_dst[s], arrived)
                nc.vector.tensor_scalar(dst_rel[:, :], dst_i[:, s, :], base_bc[:, bass.ds(g, 1)], None,
                                        ALU.subtract).then_inc(s_rel, 1)
                dve.wait_ge(s_rel, g + 1)
                nc.vector.tensor_tensor(
                    onehot[:, s, :, :], iota[:, 0:WIN].unsqueeze(1).to_broadcast([P, T, WIN]),
                    dst_rel[:, :].unsqueeze(2).to_broadcast([P, T, WIN]), ALU.is_equal).then_inc(s_oh, 1)

            def copy_inputs(g, first=False):
                dve.wait_ge(s_in_T, g + 1)
                if not first:
                    dve.wait_ge(s_z1, g)
                nc.vector.tensor_copy(xg_T[:, :], xg_ps[:, :]).then_inc(s_xgc, 1)
                nc.vector.tensor_copy(ea_T[:, :], ea_ps[:, 0:P]).then_inc(s_eac, 1)
                dve.wait_ge(s_bwin, g + 1)
                nc.vector.tensor_add(bwin_bd[0:H, 0:H], bwin_ps[0:H, 0:H], b1_bc[0:H, :])
                nc.vector.tensor_add(bwin_bd[H:P, H:P], bwin_ps[H:P, 0:H], b1_bc[H:P, :]).then_inc(s_bwc, 1)
                dve.wait_ge(s_oh_T, g + 1)
                nc.vector.tensor_copy(oh_T[:, :], oh_ps[:, :]).then_inc(s_ohc, 1)

            def add_window(g):
                at = window_start(g)
                dve.wait_ge(s_agg, g + 1)
                sums = node_T[H:P, bass.ds(at, WIN)]
                nc.vector.tensor_add(sums, sums, agg_ps[H:P, 0:WIN]).then_inc(s_added, 1)

            dve.wait_ge(s_const, 3)
            dve.wait_ge(s_w, 16 * n_weights)
            dve.wait_ge(s_xT_a, -(-len(xT_banks) // 2))
            dve.wait_ge(s_xT_v, len(xT_banks) // 2)
            general = dve.value_load(general_i[0:1, 0:1], min_val=0, max_val=1)
            with dve.If(general == 0):
                prepare(0, 0, 16)
                copy_inputs(0, first=True)
                prepare(1, 1, 16)
                with dve.Fori(0, FULL // S - 1) as k:
                    for u in range(S):
                        copy_inputs(k * S + (u + 1))
                        prepare(k * S + (u + 2), (u + 2) % S, k * 16 + 16 * ((u + 2) // S + 1))
                        add_window(k * S + u)
                for g in range(FULL - S + 1, FULL + 1):
                    copy_inputs(g)
                    if g < FULL:
                        tail = g + 1 == FULL
                        prepare(g + 1, (g + 1) % S, 16 * ((g + 1) // S + 1 + tail))
                    add_window(g - 1)
                add_window(FULL)
                dve.wait_ge(s_added, NG)
                nc.vector.memset(done_mark[:, :], 0.0).then_inc(s_sums, 1)
            with dve.Else():
                def any_group(g, loaded, columns):
                    if columns < T:
                        dve.wait_ge(a_rel, FULL * (NT + 1))
                        nc.vector.memset(dst_rel[:, columns:T], -1.0)
                    dve.wait_ge(a_load, loaded)
                    nc.vector.tensor_copy(dst_rel[:, 0:columns], dst_i[:, 0, 0:columns]).then_inc(a_rel, 1)
                    dve.wait_ge(a_T, g + 1)
                    nc.vector.tensor_copy(xg_T[:, :], xg_ps[:, :])
                    nc.vector.tensor_copy(oh_T[:, :], oh_ps[:, :])
                    nc.vector.tensor_copy(ea_T[:, :], ea_ps[:, 0:P]).then_inc(a_Tc, 1)
                    with dve.Fori(0, NT) as k:
                        step_no = g * NT + k
                        dve.wait_ge(a_rel, g * (NT + 1) + k + 1)
                        nc.vector.tensor_tensor(
                            onehot_any, iota[:, :].unsqueeze(1).to_broadcast([P, T, P]),
                            dst_rel[:, :].unsqueeze(2).to_broadcast([P, T, P]), ALU.is_equal).then_inc(a_oh, 1)
                        dve.wait_ge(a_oh, step_no + 1)
                        nc.vector.tensor_scalar(dst_rel[:, :], dst_rel[:, :], float(-P), None,
                                                ALU.add).then_inc(a_rel, 1)
                        dve.wait_ge(a_agg, step_no + 1)
                        sums = node_T[H:P, bass.ds(k * P, P)]
                        nc.vector.tensor_add(sums, sums, agg_ps[H:P, 0:P]).then_inc(a_added, 1)

                with dve.Fori(0, FULL) as g:
                    any_group(g, g * 48 + 48, T)
                any_group(FULL, FULL * 48 + 48, TT)
                dve.wait_ge(a_added, NG * NT)
                nc.vector.memset(done_mark[:, :], 0.0).then_inc(s_sums, 1)

            def sum_squares(n):
                a, b = n * OB, min(NT, n * OB + OB)
                dve.wait_ge(s_sq, n + 1)
                nc.vector.tensor_reduce(var[:, a:b], square[:, n % 2, 0:(b - a) * H].rearrange(
                    "p (k f) -> p k f", f=H), AX.X, ALU.add).then_inc(s_sqr, 1)

            for n in range(NOB):
                a, b = n * OB, min(NT, n * OB + OB)
                tiles = xs[:, a:b, :]
                dve.wait_ge(s_upd, n + 1)
                nc.vector.tensor_add(tiles, tiles, upd[:, n % 2, 0:(b - a) * H].rearrange(
                    "p (k f) -> p k f", f=H)).then_inc(s_res, 1)
                dve.wait_ge(s_res, n + 1)
                step(nc.vector.tensor_reduce(mean[:, a:b], tiles, AX.X, ALU.add))
                step(nc.vector.tensor_scalar(mean[:, a:b], mean[:, a:b], 1.0 / H, None, ALU.mult))
                nc.vector.tensor_sub(tiles, tiles, mean[:, a:b].unsqueeze(2).to_broadcast([P, b - a, H])
                                     ).then_inc(s_cen, 1)
                if n >= 1:
                    sum_squares(n - 1)
            sum_squares(NOB - 1)
            dve.wait_ge(s_sqr, NOB)
            nc.vector.tensor_scalar(var[:, :], var[:, :], 1.0 / H, EPS, ALU.mult, ALU.add).then_inc(s_var, 1)
            dve.wait_ge(s_std, 1)
            dve.wait_ge(s_cen, NOB)
            step(nc.vector.reciprocal(rstd[:, :], rstd[:, :]))
            cuts = store_cuts + [NT]
            for a, b in zip(cuts, cuts[1:]):
                nc.vector.tensor_mul(xs[:, a:b, :], xs[:, a:b, :],
                                     rstd[:, a:b].unsqueeze(2).to_broadcast([P, b - a, H])).then_inc(s_norm, 1)

        @block.tensor
        def _(pe):
            def pairs(t):
                return t.rearrange("p (j c) -> p j c", c=P)

            pe.wait_ge(s_ident, 2)
            pe.wait_ge(s_chk, 2)
            nc.tensor.matmul(z1_ps[:, 0:Q * P], ones[:, :], base_diag[:, :, :].rearrange("p q c -> p (q c)"),
                             start=True, stop=True).then_inc(s_base, 1)
            pe.wait_ge(s_chk, 5)
            nc.tensor.transpose(oh_ps[0:1, 0:P], outside[:, :], ident[:, :]).then_inc(s_out_T, 1)
            pe.wait_ge(s_flag, 1)

            pe.wait_ge(s_x, 16 * N_X)
            for n, (a, b) in enumerate(xT_banks):
                bank = (xg_ps, oh_ps)[n % 2]
                if n >= 2:
                    pe.wait_ge((s_xT_a, s_xT_v)[n % 2], n // 2)
                for j, k in enumerate(range(a, b)):
                    last = nc.tensor.transpose(bank[0:H, j * P:(j + 1) * P], xs[:, k, :], ident[:, :])
                last.then_inc(s_xT_ps, 1)

            pe.wait_ge(s_xT_a, -(-len(xT_banks) // 2))
            pe.wait_ge(s_xT_v, len(xT_banks) // 2)
            pe.wait_ge(s_w, 16 * n_weights)

            def transpose_inputs(g, s, gathered, ea_arrived):
                pe.wait_ge(s_xg[s], gathered)
                for j in range(T // 2):
                    nc.tensor.transpose(xg_ps[:, j * P:(j + 1) * P],
                                        xg[:, s, 2 * j:2 * j + 2, :].rearrange("p t f -> p (t f)"), ident[:, :])
                pe.wait_ge(s_ea[s], ea_arrived)
                nc.tensor.transpose(ea_ps[:, 0:P], ea[:, s, :], ident[:, :]).then_inc(s_in_T, 1)
                pe.wait_ge(s_xwin, g + 1)
                nc.tensor.matmul(bwin_ps[:, 0:H], xwin[:, :, :].rearrange("p a n -> p (a n)"), w1b_bd[0:H, 0:H],
                                 start=True, stop=True).then_inc(s_bwin, 1)
                pe.wait_ge(s_oh, g + 1)
                for j in range(T // 2):
                    last = nc.tensor.transpose(oh_ps[:, j * P:(j + 1) * P],
                                               onehot[:, s, 2 * j:2 * j + 2, :].rearrange("p t n -> p (t n)"),
                                               ident[:, :])
                last.then_inc(s_oh_T, 1)

            def first_layer(g):
                pe.wait_ge(s_ohc, g + 1)
                nc.tensor.matmul(z1_ps[:, :], ea_T[:, :], w1c_bd[:, :], start=True, stop=False)
                for j in range(T // 2):
                    c = slice(j * P, (j + 1) * P)
                    nc.tensor.matmul(z1_ps[:, c], xg_T[:, c], w1a_bd[:, :], start=False, stop=False)
                    last = nc.tensor.matmul(z1_ps[:, c], oh_T[:, c], bwin_bd[:, :], start=False,
                                            stop=(j == T // 2 - 1))
                last.then_inc(s_z1, 1)

            def transpose_h(g):
                pe.wait_ge(s_h, g + 1)
                for j in range(T // 2):
                    c = slice(j * P, (j + 1) * P)
                    last = nc.tensor.transpose(h_ps[:, c], h[:, c], ident[:, :])
                last.then_inc(s_hT, 1)

            def second_layer(g):
                pe.wait_ge(s_hTc, g + 1)
                for j in range(T // 2):
                    c = slice(j * P, (j + 1) * P)
                    nc.tensor.matmul(z2_ps[:, c], h_T[:, c], w2_bd[:, :], start=(j == 0), stop=False)
                nc.tensor.matmul(z2_ps[:, :], ones[0:1, :], b2_rep[:, :], start=False, stop=True).then_inc(s_z2, 1)

            def sum_window(g, s):
                pe.wait_ge(s_msg, g + 1)
                for t in range(T):
                    last = nc.tensor.matmul(agg_ps[H:P, 0:WIN], msg[:, s, t * H:(t + 1) * H], onehot[:, s, t, :],
                                            start=(t == 0), stop=(t == T - 1))
                last.then_inc(s_agg, 1)

            general = pe.value_load(general_i[0:1, 0:1], min_val=0, max_val=1)
            with pe.If(general == 0):
                transpose_inputs(0, 0, 16 * T, 16)
                first_layer(0)
                transpose_h(0)
                with pe.Fori(0, FULL // S - 1) as k:
                    for u in range(S):
                        g, s, uses = k * S + (u + 1), (u + 1) % S, (u + 1) // S + 1
                        transpose_inputs(g, s, k * (16 * T) + 16 * T * uses, k * 16 + 16 * uses)
                        second_layer(k * S + u)
                        first_layer(g)
                        sum_window(k * S + u, u)
                        transpose_h(g)
                for g in range(FULL - S + 1, FULL + 1):
                    uses = g // S
                    transpose_inputs(g, g % S, 16 * (T * uses + (TT if g == FULL else T)), 16 * uses + 16)
                    second_layer(g - 1)
                    first_layer(g)
                    sum_window(g - 1, (g - 1) % S)
                    transpose_h(g)
                second_layer(FULL)
                pe.wait_ge(s_added, FULL)
                sum_window(FULL, FULL % S)
            with pe.Else():
                def any_group(g, gathered):
                    pe.wait_ge(a_xs, gathered)
                    pe.wait_ge(a_xd, gathered)
                    for rows_of, bank in ((SRC, xg_ps), (DST, oh_ps)):
                        for j in range(T // 2):
                            nc.tensor.transpose(bank[:, j * P:(j + 1) * P],
                                                xg[:, rows_of, 2 * j:2 * j + 2, :].rearrange("p t f -> p (t f)"),
                                                ident[:, :])
                    nc.tensor.transpose(ea_ps[:, 0:P], ea[:, 0, :], ident[:, :]).then_inc(a_T, 1)
                    pe.wait_ge(a_Tc, g + 1)
                    nc.tensor.matmul(z1_ps[:, :], ea_T[:, :], w1c_bd[:, :], start=True, stop=False)
                    for j in range(T // 2):
                        c = slice(j * P, (j + 1) * P)
                        nc.tensor.matmul(z1_ps[:, c], xg_T[:, c], w1a_bd[:, :], start=False, stop=False)
                        nc.tensor.matmul(z1_ps[:, c], oh_T[:, c], w1b_bd[:, :], start=False, stop=False)
                    nc.tensor.matmul(z1_ps[:, :], ones[0:1, :], b1_rep[:, :], start=False, stop=True).then_inc(a_z1, 1)
                    pe.wait_ge(a_h, g + 1)
                    for j in range(T // 2):
                        c = slice(j * P, (j + 1) * P)
                        last = nc.tensor.transpose(h_ps[:, c], h[:, c], ident[:, :])
                    last.then_inc(a_hT, 1)
                    pe.wait_ge(a_hTc, g + 1)
                    for j in range(T // 2):
                        c = slice(j * P, (j + 1) * P)
                        nc.tensor.matmul(z2_ps[:, c], h_T[:, c], w2_bd[:, :], start=(j == 0), stop=False)
                    nc.tensor.matmul(z2_ps[:, :], ones[0:1, :], b2_rep[:, :], start=False, stop=True).then_inc(a_z2, 1)
                    pe.wait_ge(a_msg, g + 1)
                    pe.nop(nofuse=True)
                    with pe.Fori(0, NT) as k:
                        pe.wait_ge(a_oh, g * NT + k + 1)
                        for t in range(T):
                            last = nc.tensor.matmul(agg_ps[H:P, 0:P], msg[:, 0, t * H:(t + 1) * H],
                                                    onehot_any[:, t, :], start=(t == 0), stop=(t == T - 1))
                        last.then_inc(a_agg, 1)

                with pe.Fori(0, FULL) as g:
                    any_group(g, g * (16 * T) + 16 * T)
                any_group(FULL, 16 * (T * FULL + TT))

            pe.wait_ge(s_sums, 1)
            for n in range(NOB):
                z = (z1_ps, z2_ps)[n % 2]
                a, b = n * OB, min(NT, n * OB + OB)
                if n >= 2:
                    pe.wait_ge(s_upd, n - 1)
                for j, k in enumerate(range(a, b)):
                    nc.tensor.matmul(z[:, j * H:(j + 1) * H], node_T[:, k * P:(k + 1) * P], w3[:, :],
                                     start=(j == 0), stop=False)
                m = (b - a) * H
                nc.tensor.matmul(z[:, 0:m], ones[0:1, :], b3_rep[:, 0:m], start=False, stop=True).then_inc(s_z3, 1)


_INS = ["x", "src", "dst", "edge_attr_16", "L0_gnn_W1", "L0_gnn_b1", "L0_gnn_W2", "L0_gnn_b2", "L0_gnn_W3", "L0_gnn_b3"]


def kernel(**inputs):
    import numpy as _np
    import concourse.bacc as _bacc
    from concourse import mybir as _mybir
    from concourse.bass_utils import run_bass_kernel_spmd as _run

    nc = _bacc.Bacc("TRN2", target_bir_lowering=False, num_devices=1)
    arrays, args = {}, []
    for name in _INS:
        a = _np.ascontiguousarray(inputs[name])
        arrays[f"in_{name}_dram"] = a
        args.append(nc.dram_tensor(f"in_{name}_dram", a.shape, _mybir.dt.from_np(a.dtype), kind="ExternalInput").ap())
    out = nc.dram_tensor("out_0_dram", inputs["x"].shape, _mybir.dt.float32, kind="ExternalOutput").ap()
    gnn_layer(nc, *args, out)
    r = _run(nc, [arrays], core_ids=[0])
    return r.results[0]["out_0_dram"]
```

```python
import concourse.bass as bass
import concourse.mybir as mybir
from contextlib import ExitStack


def gnn_layer(nc, x, src, dst, edge_attr, W1, b1, W2, b2, W3, b3, out):
    F32, I32, BF16 = mybir.dt.float32, mybir.dt.int32, mybir.dt.bfloat16
    ALU, ACT, AX = mybir.AluOpType, mybir.ActivationFunctionType, mybir.AxisListType

    P = 128
    N, H = x.shape
    E, D = edge_attr.shape
    T = 8
    HT = T // 2
    G = P * T
    FULL = E // G
    TT = (E - FULL * G) // P
    assert 0 < TT < T and E == FULL * G + TT * P and 2 * H == P and T * D == P
    NG = FULL + 1
    WIN = P - H - D
    LASTW = N - WIN
    OH, XS, EA = slice(0, WIN), slice(WIN, WIN + H), slice(WIN + H, P)
    NT = -(-N // P)
    NPAD = NT * P
    N0 = (NT - 1) * P
    NREM = N - N0
    S = 6
    assert FULL % S == 0
    REST = FULL - S + 1
    QF = FULL // P
    QR = FULL - QF * P
    Q = QF + 1
    EPS = 1e-5
    C = HT * P
    NB = 4
    ITERS = 4
    SPAN = ITERS * S
    SEGS = (FULL // S - 1) // ITERS
    LT = SPAN * G * N // (E * P)
    LN = LT * P
    LOTS = SEGS - 1
    LAST_T = NT - LOTS * LT
    assert SEGS * ITERS == FULL // S - 1 and LN % SPAN == 0 and LT % 2 == 0 and LAST_T == T and LT < T
    HS = S // 2
    PICKED = T - 1
    FIRST = ITERS + 1
    PARTS = 3
    SPLIT = NT // SPAN
    HB = C // H
    ROUNDS = -(-NT // HB)
    AFTER_INPUTS, AFTER_SECOND, AFTER_FIRST, AFTER_EDGES, AFTER_SUMS = range(5)
    BESIDE = [((), (), (), (0,), (1, 2)), ((3,), (4,), (5,), (6,), (7,)), ((8,), (9,), (10,), (11,), (12,))]
    assert HS == len(BESIDE) and ROUNDS == 13 and NT <= P
    SRC, DST, ANY = 0, 1, 2

    ctx = ExitStack()
    with ctx:
        def sb(name, shape, dt=F32):
            return ctx.enter_context(nc.sbuf_tensor(name, shape, dt))

        def pb(name):
            return ctx.enter_context(nc.psum_tensor(name, [P, C], F32))

        def sem(name):
            return ctx.enter_context(nc.semaphore(name))

        node_T = sb("node_T", [P, NPAD])
        xs = sb("xs", [P, NT, H])
        ident = sb("ident", [P, P])
        iota = sb("iota", [P, P])
        ones = sb("ones", [P, P])
        zero_col = sb("zero_col", [P, 1])
        w_in = sb("w_in", [P, H])
        w_dst = sb("w_dst", [P, H])
        w1b = sb("w1b", [H, H])
        w2_bd = sb("w2_bd", [P, P])
        w3 = sb("w3", [P, H])
        b1_col = sb("b1_col", [P, 1])
        b2_col = sb("b2_col", [P, 1])
        b3_col = sb("b3_col", [P, 1])
        base_bc = sb("base_bc", [P, Q * P])
        base_i = sb("base_i", [1, Q * P], I32)
        no_node = sb("no_node", [P, T], I32)
        dst_g = sb("dst_g", [P, Q, G], I32)
        hi = sb("hi", [P, Q])
        lo = sb("lo", [P, Q])
        base_g = sb("base_g", [P, Q])
        base_diag = sb("base_diag", [P, Q, P])
        early = sb("early", [P, Q])
        outside = sb("outside", [P, 2])
        outside_all = sb("outside_all", [2, 1])
        flags_i = sb("flags_i", [2, 1], I32)
        parts = sb("parts", [P, PARTS, NT, H], BF16)
        rest = sb("rest", [P, SPLIT, H])
        place_i = sb("place_i", [P, 2], I32)
        place = sb("place", [P, 2])
        hot_row = sb("hot_row", [P, P])
        hot_tile = sb("hot_tile", [P, NT], I32)
        kept = sb("kept", [P, HB, H])
        rows_T = sb("rows_T", [P, P], BF16)
        src_i = sb("src_i", [P, S, T], I32)
        dst_i = sb("dst_i", [P, S, T], I32)
        ea = sb("ea", [P, S, T, D])
        edge_in = sb("edge_in", [P, S, T, P])
        dst_rel = sb("dst_rel", [P, T])
        xwin = sb("xwin", [H, WIN])
        in_T = sb("in_T", [P, 2, C])
        h_T = sb("h_T", [P, C])
        msg_T = sb("msg_T", [P, C])
        msg = sb("msg", [P, HT, 2, H])
        lot_T = sb("lot_T", [P, LN])
        upd_T = sb("upd_T", [P, C])
        y = sb("y", [P, T, H])
        square = sb("square", [P, T, H])
        result = sb("result", [P, T, H])
        total = sb("total", [P, T])
        var = sb("var", [P, T])
        rstd = sb("rstd", [P, T])
        done_mark = sb("done_mark", [1, 1])

        in_ps = [pb("in_ps0"), pb("in_ps1")]
        z1_ps = pb("z1_ps")
        z2_ps = pb("z2_ps")
        msg_ps = pb("msg_ps")
        agg_ps = pb("agg_ps")
        pick_ps = [pb("pick_ps0"), pb("pick_ps1")]
        upd_ps = pick_ps[1]

        s_zeroed = sem("zeroed")
        s_ident = sem("ident_made")
        s_const = sem("iota_made")
        s_dst_g = sem("dst_g_loaded")
        s_x = sem("x_loaded")
        s_w = sem("weights_loaded")
        s_chk = sem("check_step")
        s_base = sem("base_spread")
        s_out_T = sem("outside_transposed")
        s_flag = sem("general_known")
        s_sum0 = sem("sums_cleared")
        s_xT_ps = sem("x_transposed")
        s_xT_a = sem("x_T_copied_act")
        s_xT_v = sem("x_T_copied_dve")
        s_src = [sem(f"src_loaded{s}") for s in range(S)]
        s_dst = [sem(f"dst_loaded{s}") for s in range(S)]
        s_ea = [sem(f"ea_loaded{s}") for s in range(S)]
        s_xg = [sem(f"x_gathered{s}") for s in range(S)]
        s_eac = sem("ea_placed")
        s_xwin = sem("window_copied")
        s_rel = sem("dst_rel_made")
        s_oh = sem("onehot_made")
        s_in_T = sem("edge_in_transposed")
        s_bwin = sem("window_projected")
        s_in0c = sem("first_half_copied")
        s_in1c = sem("second_half_copied")
        s_bwc = sem("window_placed")
        s_z1 = sem("z1_done")
        s_h = sem("h_done")
        s_z2 = sem("z2_done")
        s_msgT = sem("messages_done")
        s_msg = sem("messages_transposed")
        s_msgc = sem("messages_copied")
        s_agg = sem("window_summed")
        s_added = sem("window_added")
        s_split = sem("split_step")
        s_place = sem("src_placed")
        s_hot = sem("hot_made")
        s_hotT = sem("hot_row_transposed")
        s_rowsT = sem("rows_T_made")
        s_round = sem("round_done")
        s_picked = sem("rows_picked")
        s_row = sem("picked_tile_made")
        a_clear = sem("any_cleared")
        a_load = sem("any_loaded")
        a_gath = [sem("any_x_src_gathered"), sem("any_x_dst_gathered")]
        a_eac = sem("any_ea_placed")
        a_rel = sem("any_dst_rel_made")
        a_T = sem("any_edge_in_transposed")
        a_Tc = sem("any_edge_in_copied")
        a_z1 = sem("any_z1_done")
        a_h = sem("any_h_done")
        a_z2 = sem("any_z2_done")
        a_msgT = sem("any_messages_done")
        a_msg = sem("any_messages_transposed")
        a_msgc = sem("any_messages_copied")
        a_oh = sem("any_onehot_made")
        a_agg = sem("any_tile_summed")
        a_added = sem("any_tile_added")
        s_sums = sem("sums_complete")
        s_lot = sem("lot_copied")
        s_z3 = sem("z3_done")
        s_upd = sem("update_done")
        s_updT = sem("update_transposed")
        s_res = sem("residual_added")
        s_tot = sem("features_summed")
        s_cen = sem("centred")
        s_sq = sem("squared")
        s_sqr = sem("squares_summed")
        s_var = sem("variance_done")
        s_std = sem("std_done")
        s_rstd = sem("rstd_done")
        s_norm = sem("normalised")
        s_out = sem("out_stored")

        block = ctx.enter_context(nc.Block())

        src_v = src[0:FULL * G].rearrange("(g p t) -> g p t", p=P, t=T)
        dst_v = dst[0:FULL * G].rearrange("(g p t) -> g p t", p=P, t=T)
        ea_v = edge_attr[0:FULL * G, :].rearrange("(g p t) d -> g p t d", p=P, t=T)
        src_tail = src[FULL * G:E].rearrange("(p t) -> p t", t=TT)
        dst_tail = dst[FULL * G:E].rearrange("(p t) -> p t", t=TT)
        ea_tail = edge_attr[FULL * G:E, :].rearrange("(p t) d -> p t d", t=TT)
        n_weights = 5 + 2 + 6
        xT_banks = [(k, min(k + NB, NT)) for k in range(0, NT, NB)]
        def row(w):
            return w.rearrange("(a n) -> a n", a=1)

        def column(w):
            return w.rearrange("(n a) -> n a", a=1)

        def halves(m, psum):
            if psum:
                return upd_ps[:, 0:m * H].rearrange("p (c a f) -> p a c f", a=2, f=H)
            return y[:, 0:m, :].rearrange("p (a c) f -> p a c f", a=2)

        @block.sync
        def _(sp):
            def load_rest(n, g, s):
                sp.dma_start(dst_i[:, s, :], dst_v[g]).then_inc(s_dst[s], 16)
                sp.dma_start(ea[:, s, :, :], ea_v[g]).then_inc(s_ea[s], 16)

            for g in range(S):
                sp.dma_start(src_i[:, g, :], src_v[g]).then_inc(s_src[g], 16)
            sp.dma_start(dst_g[:, 0:QF, :],
                         dst[0:QF * P * G].rearrange("(q p e) -> p q e", p=P, e=G)).then_inc(s_dst_g, 16)
            sp.wait_ge(s_zeroed, 1)
            sp.dma_start(dst_g[0:QR, QF, :],
                         dst[QF * P * G:FULL * G].rearrange("(p e) -> p e", e=G)).then_inc(s_dst_g, 16)
            sp.dma_start(dst_g[QR:QR + 1, QF, 0:TT * P], row(dst[FULL * G:E])).then_inc(s_dst_g, 16)
            sp.dma_start(dst_g[QR:QR + 1, QF, TT * P:G],
                         row(dst[FULL * G:FULL * G + G - TT * P])).then_inc(s_dst_g, 16)
            sp.dma_start(xs[:, 0:NT - 1, :],
                         x[0:N0, :].rearrange("(k p) f -> p k f", p=P)).then_inc(s_x, 16)
            sp.wait_ge(s_zeroed, 2)
            sp.dma_start(xs[0:NREM, NT - 1, :], x[N0:N, :]).then_inc(s_x, 16)
            sp.wait_ge(s_flag, 1)
            general = sp.value_load(flags_i[0:1, 0:1], min_val=0, max_val=1)
            with sp.If(general == 0):
                for g in range(S):
                    load_rest(0, g, g)
                with sp.Fori(1, FULL // S) as k:
                    for s in range(S):
                        sp.wait_ge(s_rel, k * S + (s - S + 1))
                        sp.wait_ge(s_in_T, k * S + (s - S + 1))
                        sp.nop(nofuse=True)
                        sp.dma_start(src_i[:, s, :], src_v[k * S + s]).then_inc(s_src[s], 16)
                        load_rest(k, k * S + s, s)
                sp.wait_ge(s_rel, FULL - S + 1)
                sp.wait_ge(s_in_T, FULL - S + 1)
                sp.dma_start(src_i[:, 0, 0:TT], src_tail).then_inc(s_src[0], 16)
                sp.dma_start(dst_i[:, 0, 0:TT], dst_tail).then_inc(s_dst[0], 16)
                sp.dma_start(dst_i[:, 0, TT:T], no_node[:, TT:T]).then_inc(s_dst[0], 16)
                sp.dma_start(ea[:, 0, 0:TT, :], ea_tail).then_inc(s_ea[0], 16)
            with sp.Else():
                sp.wait_ge(a_clear, 1)

                def load_any(g):
                    sp.dma_start(src_i[:, 0, :], src_v[g]).then_inc(a_load, 16)
                    sp.dma_start(dst_i[:, 0, :], dst_v[g]).then_inc(a_load, 16)
                    sp.dma_start(ea[:, 0, :, :], ea_v[g]).then_inc(a_load, 16)

                load_any(0)
                with sp.Fori(1, FULL) as g:
                    sp.wait_ge(a_added, g * NT)
                    sp.nop(nofuse=True)
                    load_any(g)
                sp.wait_ge(a_added, FULL * NT)
                sp.dma_start(src_i[:, 0, 0:TT], src_tail).then_inc(a_load, 16)
                sp.dma_start(dst_i[:, 0, 0:TT], dst_tail).then_inc(a_load, 16)
                sp.dma_start(ea[:, 0, 0:TT, :], ea_tail).then_inc(a_load, 16)
            sp.wait_ge(s_out, 16 * (LOTS + 2))

        @block.gpsimd
        def _(pool):
            nc.gpsimd.memset(ident[:], 0.0).then_inc(s_ident, 1)
            pool.wait_ge(s_ident, 1)
            nc.gpsimd.affine_select(out=ident[:], in_=ident[:], compare_op=ALU.not_equal, fill=1.0, base=0,
                                    pattern=[[-1, P]], channel_multiplier=1).then_inc(s_ident, 1)
            nc.gpsimd.iota(iota[:], pattern=[[1, P]], base=0, channel_multiplier=0,
                           allow_small_or_imprecise_dtypes=True).then_inc(s_const, 1)
            nc.gpsimd.iota(early[:], pattern=[[P * (LN // SPAN), Q]], base=-LN, channel_multiplier=LN // SPAN,
                           allow_small_or_imprecise_dtypes=True).then_inc(s_const, 1)

            def gather(indices, from_slot, to_slot, tiles, arrived):
                for t in range(tiles):
                    pool.indirect_dma_start(
                        out=edge_in[:, to_slot, t, XS], out_offset=None, in_=x[:, :],
                        in_offset=bass.IndirectOffsetOnAxis(ap=indices[:, from_slot, t:t + 1], axis=0),
                    ).then_inc(arrived, 16)

            for s in range(S):
                pool.wait_ge(s_src[s], 16)
                gather(src_i, s, s, T, s_xg[s])
            pool.wait_ge(s_flag, 1)
            general = pool.value_load(flags_i[0:1, 0:1], min_val=0, max_val=1)
            with pool.If(general == 0):
                def fill_slots(k, tiles):
                    for s in range(S):
                        pool.wait_ge(s_in_T, k * S + (s - S + 1))
                        pool.wait_ge(s_src[s], k * 16 + 16)
                        pool.nop(nofuse=True)
                        gather(src_i, s, s, T if s % HS else tiles, s_xg[s])

                with pool.Fori(1, FIRST) as k:
                    fill_slots(k, T)
                with pool.Fori(FIRST, FULL // S) as k:
                    fill_slots(k, PICKED)
                pool.wait_ge(s_in_T, FULL - S + 1)
                pool.wait_ge(s_src[0], 16 * (FULL // S + 1))
                gather(src_i, 0, 0, TT, s_xg[0])
            with pool.Else():
                def gather_both(tiles):
                    gather(src_i, 0, SRC, tiles, a_gath[SRC])
                    gather(dst_i, 0, DST, tiles, a_gath[DST])

                with pool.Fori(0, FULL) as g:
                    pool.wait_ge(a_load, g * 48 + 48)
                    pool.nop(nofuse=True)
                    gather_both(T)
                pool.wait_ge(a_load, FULL * 48 + 48)
                gather_both(TT)

        @block.scalar
        def _(act):
            act.wait_ge(s_zeroed, 2)
            loads = [(w_in[XS, :], W1[0:H, :]), (w_in[EA, :], W1[2 * H:2 * H + D, :]),
                     (w_dst[XS, :], W1[H:2 * H, :]), (w1b[:, :], W1[H:2 * H, :]), (w3[:, :], W3),
                     (w2_bd[0:H, 0:H], W2), (w2_bd[H:P, H:P], W2)]
            for col, b in ((b1_col, b1), (b2_col, b2), (b3_col, b3)):
                loads += [(col[0:H, :], column(b)), (col[H:P, :], column(b))]
            for to, of in loads:
                act.dma_start(to, of).then_inc(s_w, 16)
            nc.scalar.copy(node_T[H:P, :], zero_col[H:P, :].to_broadcast([H, NPAD])).then_inc(s_sum0, 1)

            for n in range(0, len(xT_banks), 2):
                a, b = xT_banks[n]
                act.wait_ge(s_xT_ps, n + 1)
                nc.scalar.copy(node_T[0:H, a * P:b * P], in_ps[0][0:H, 0:(b - a) * P]).then_inc(s_xT_a, 1)

            def place_ea(s, arrived):
                act.wait_ge(s_ea[s], arrived)
                nc.scalar.copy(edge_in[:, s, :, EA], ea[:, s, :, :]).then_inc(s_eac, 1)

            def copy_second_half(g):
                act.wait_ge(s_in_T, g + 1)
                nc.scalar.copy(in_T[:, 1, :], in_ps[1][:, :]).then_inc(s_in1c, 1)

            def first_silu(g):
                act.wait_ge(s_z1, g + 1)
                nc.scalar.activation(h_T[:, :], z1_ps[:, :], ACT.Silu, bias=b1_col[:, :]).then_inc(s_h, 1)

            def second_silu(g):
                act.wait_ge(s_z2, g + 1)
                nc.scalar.activation(msg_T[:, :], z2_ps[:, :], ACT.Silu, bias=b2_col[:, :]).then_inc(s_msgT, 1)

            act.wait_ge(s_w, 16 * n_weights)
            act.wait_ge(s_flag, 1)
            general = act.value_load(flags_i[0:1, 0:1], min_val=0, max_val=1)
            late = act.value_load(flags_i[1:2, 0:1], min_val=0, max_val=1)

            def update_lot(b, m, store):
                act.wait_ge(s_z3, b + 1)
                nc.scalar.activation(upd_T[:, 0:m * H], z2_ps[:, 0:m * H], ACT.Silu, bias=b3_col[:, :]).then_inc(s_upd, 1)
                act.wait_ge(s_var, b + 1)
                nc.scalar.activation(rstd[:, 0:m], var[:, 0:m], ACT.Sqrt).then_inc(s_std, 1)
                act.wait_ge(s_norm, b + 1)
                act.nop(nofuse=True)
                store()

            def inner_lot(b):
                nc.scalar.copy(lot_T[:, :], node_T[:, bass.ds(b * LN, LN)]).then_inc(s_lot, 1)
                update_lot(b, LT, lambda: act.dma_start(
                    out[bass.ds(b * LN, LN), :].rearrange("(k p) f -> p k f", p=P), result[:, 0:LT, :]).then_inc(s_out, 16))
                act.wait_ge(s_out, b * 16 + 16)
                act.nop(nofuse=True)

            def last_lot():
                a = LOTS * LT
                act.dma_start(out[a * P:N0, :].rearrange("(k p) f -> p k f", p=P),
                              result[:, 0:NT - 1 - a, :]).then_inc(s_out, 16)
                act.dma_start(out[N0:N, :], result[0:NREM, NT - 1 - a, :]).then_inc(s_out, 16)

            with act.If(general == 0):
                place_ea(0, 16)
                copy_second_half(0)
                first_silu(0)
                place_ea(1, 16)

                def groups(k):
                    for u in range(S):
                        copy_second_half(k * S + (u + 1))
                        second_silu(k * S + u)
                        first_silu(k * S + (u + 1))
                        place_ea((u + 2) % S, k * 16 + 16 * ((u + 2) // S + 1))

                with act.Fori(0, ITERS) as k:
                    groups(k)
                with act.Fori(0, LOTS) as b:
                    with act.Fori(0, ITERS) as i:
                        groups(b * ITERS + i + ITERS)
                    with act.If(late == 0):
                        act.wait_ge(s_added, b * SPAN + 2 * SPAN)
                        inner_lot(b)
                for g in range(REST, NG):
                    copy_second_half(g)
                    second_silu(g - 1)
                    first_silu(g)
                    if g < FULL:
                        place_ea((g + 1) % S, 16 * ((g + 1) // S + 1))
                second_silu(FULL)
            with act.Else():
                def any_group(g, loaded, tiles):
                    act.wait_ge(a_load, loaded)
                    nc.scalar.copy(edge_in[:, SRC, 0:tiles, EA], ea[:, 0, 0:tiles, :]).then_inc(a_eac, 1)
                    act.wait_ge(a_z1, g + 1)
                    nc.scalar.activation(h_T[:, :], z1_ps[:, :], ACT.Silu, bias=b1_col[:, :]).then_inc(a_h, 1)
                    act.wait_ge(a_z2, g + 1)
                    nc.scalar.activation(msg_T[:, :], z2_ps[:, :], ACT.Silu, bias=b2_col[:, :]).then_inc(a_msgT, 1)

                act.wait_ge(a_clear, 1)
                with act.Fori(0, FULL) as g:
                    any_group(g, g * 48 + 48, T)
                any_group(FULL, FULL * 48 + 48, TT)

            with act.If(late == 1):
                act.wait_ge(s_sums, 1)
                with act.Fori(0, LOTS) as b:
                    inner_lot(b)
            update_lot(LOTS, LAST_T, last_lot)

        @block.vector
        def _(dve):
            steps = [0]

            def step(ins):
                ins.then_inc(s_chk, 1)
                steps[0] += 1
                dve.wait_ge(s_chk, steps[0])

            nc.vector.memset(dst_g[:, QF, :], N - 1).then_inc(s_zeroed, 1)
            nc.vector.memset(w_dst[:, :], 0.0)
            nc.vector.memset(w_in[OH, :], 0.0)
            nc.vector.memset(w2_bd[:, :], 0.0)
            nc.vector.memset(zero_col[:, :], 0.0)
            nc.vector.memset(no_node[:, :], -1)
            nc.vector.memset(ones[:, :], 1.0)
            nc.vector.memset(xs[:, NT - 1, :], 0.0).then_inc(s_zeroed, 1)

            dve.wait_ge(s_dst_g, 4 * 16)
            nc.vector.tensor_reduce(hi[:, :], dst_g[:, :, :], AX.X, ALU.max)
            nc.vector.tensor_reduce(lo[:, :], dst_g[:, :, :], AX.X, ALU.min)
            step(nc.vector.tensor_scalar(base_g[:, :], dst_g[:, :, 0], float(LASTW), None, ALU.min))
            dve.wait_ge(s_ident, 2)
            for q in range(Q):
                last = nc.vector.tensor_scalar(base_diag[:, q, :], ident[:, :], base_g[:, q:q + 1], None, ALU.mult)
            step(last)
            dve.wait_ge(s_const, 2)
            nc.vector.tensor_sub(hi[:, :], hi[:, :], base_g[:, :])
            nc.vector.tensor_scalar(early[:, :], early[:, :], float(LN // SPAN * FULL - LN), None, ALU.min)
            step(nc.vector.tensor_sub(lo[:, :], base_g[:, :], lo[:, :]))
            nc.vector.tensor_sub(early[:, :], early[:, :], base_g[:, :])
            step(nc.vector.scalar_tensor_tensor(out=hi[:, :], in0=hi[:, :], scalar=float(1 - WIN), in1=lo[:, :],
                                                op0=ALU.add, op1=ALU.max))
            nc.vector.tensor_reduce(outside[:, 0:1], hi[:, :], AX.X, ALU.max)
            step(nc.vector.tensor_tensor(early[:, :], early[:, :], hi[:, :], ALU.max))
            step(nc.vector.tensor_reduce(outside[:, 1:2], early[:, :], AX.X, ALU.max))
            dve.wait_ge(s_out_T, 1)
            step(nc.vector.tensor_reduce(outside_all[:, :], z2_ps[0:2, 0:P], AX.X, ALU.max))
            nc.vector.tensor_scalar(flags_i[:, :], outside_all[:, :], 0.0, None, ALU.is_gt).then_inc(s_flag, 1)
            dve.wait_ge(s_base, 1)
            nc.vector.tensor_copy(base_bc[:, :], z1_ps[:, 0:Q * P])
            step(nc.vector.tensor_copy(base_i[:, :], z1_ps[0:1, 0:Q * P]))

            for n in range(1, len(xT_banks), 2):
                a, b = xT_banks[n]
                dve.wait_ge(s_xT_ps, n + 1)
                nc.vector.tensor_copy(node_T[0:H, a * P:b * P], in_ps[1][0:H, 0:(b - a) * P]).then_inc(s_xT_v, 1)

            def window_start(g):
                return dve.value_load(base_i[0:1, bass.ds(g, 1)], min_val=0, max_val=LASTW)

            def prepare(g, s, arrived):
                at = window_start(g)
                nc.vector.tensor_scalar(xwin[:, :], node_T[0:H, bass.ds(at, WIN)], 1.0, None,
                                        ALU.mult).then_inc(s_xwin, 1)
                dve.wait_ge(s_dst[s], arrived)
                nc.vector.tensor_scalar(dst_rel[:, :], dst_i[:, s, :], base_bc[:, bass.ds(g, 1)], None,
                                        ALU.subtract).then_inc(s_rel, 1)
                dve.wait_ge(s_rel, g + 1)
                nc.vector.tensor_tensor(
                    edge_in[:, s, :, OH], iota[:, OH].unsqueeze(1).to_broadcast([P, T, WIN]),
                    dst_rel[:, :].unsqueeze(2).to_broadcast([P, T, WIN]), ALU.is_equal).then_inc(s_oh, 1)

            def copy_inputs(g, first=False):
                if not first:
                    dve.wait_ge(s_z1, g)
                dve.wait_ge(s_in_T, g + 1)
                nc.vector.tensor_copy(in_T[:, 0, :], in_ps[0][:, :]).then_inc(s_in0c, 1)
                dve.wait_ge(s_bwin, g + 1)
                nc.vector.tensor_copy(w_in[OH, :], agg_ps[OH, 0:H]).then_inc(s_bwc, 1)

            def add_messages(g, beside=None):
                dve.wait_ge(s_msg, g + 1)
                nc.vector.tensor_copy(msg[:, :, :, :].rearrange("p c a f -> p (c a f)"), msg_ps[:, :]).then_inc(s_msgc, 1)
                if beside:
                    beside()
                at = window_start(g)
                dve.wait_ge(s_agg, g + 1)
                sums = node_T[H:P, bass.ds(at, WIN)]
                nc.vector.tensor_add(sums, sums, agg_ps[H:P, OH]).then_inc(s_added, 1)

            dve.wait_ge(s_const, 1)
            dve.wait_ge(s_sum0, 1)
            dve.wait_ge(s_xT_a, -(-len(xT_banks) // 2))
            dve.wait_ge(s_xT_v, len(xT_banks) // 2)
            general = dve.value_load(flags_i[0:1, 0:1], min_val=0, max_val=1)
            late = dve.value_load(flags_i[1:2, 0:1], min_val=0, max_val=1)

            def update_lot(b, m, tiles):
                lot, rows = y[:, 0:m, :], total[:, 0:m]
                dve.wait_ge(s_updT, b + 1)
                nc.vector.tensor_add(halves(m, False), tiles.rearrange("p (a c) f -> p a c f", a=2),
                                     halves(m, True)).then_inc(s_res, 1)
                dve.wait_ge(s_res, b + 1)
                nc.vector.tensor_reduce(rows, lot, AX.X, ALU.add).then_inc(s_tot, 1)
                dve.wait_ge(s_tot, b + 1)
                nc.vector.scalar_tensor_tensor(out=lot, in0=rows.unsqueeze(2).to_broadcast([P, m, H]), scalar=-1.0 / H,
                                               in1=lot, op0=ALU.mult, op1=ALU.add).then_inc(s_cen, 1)
                dve.wait_ge(s_cen, b + 1)
                nc.vector.tensor_mul(square[:, 0:m, :], lot, lot).then_inc(s_sq, 1)
                dve.wait_ge(s_sq, b + 1)
                nc.vector.tensor_reduce(var[:, 0:m], square[:, 0:m, :], AX.X, ALU.add).then_inc(s_sqr, 1)
                dve.wait_ge(s_sqr, b + 1)
                nc.vector.tensor_scalar(var[:, 0:m], var[:, 0:m], 1.0 / H, EPS, ALU.mult, ALU.add).then_inc(s_var, 1)
                dve.wait_ge(s_std, b + 1)
                nc.vector.reciprocal(rstd[:, 0:m], rstd[:, 0:m]).then_inc(s_rstd, 1)
                dve.wait_ge(s_rstd, b + 1)
                nc.vector.tensor_mul(result[:, 0:m, :], lot,
                                     rstd[:, 0:m].unsqueeze(2).to_broadcast([P, m, H])).then_inc(s_norm, 1)

            def inner_lot(b):
                update_lot(b, LT, xs[:, bass.ds(b * LT, LT), :])

            with dve.If(general == 0):
                prepare(0, 0, 16)
                copy_inputs(0, first=True)
                prepare(1, 1, 16)

                def split(n, at, tiles):
                    of, left = xs[:, bass.ds(at, tiles), :], rest[:, 0:tiles, :]
                    first, second, third = (parts[:, i, bass.ds(at, tiles), :] for i in range(PARTS))
                    nc.vector.tensor_copy(first, of).then_inc(s_split, 1)
                    dve.wait_ge(s_split, n * 4 + 1)
                    nc.vector.tensor_sub(left, of, first).then_inc(s_split, 1)
                    dve.wait_ge(s_split, n * 4 + 2)
                    nc.vector.tensor_copy(second, left).then_inc(s_split, 1)
                    dve.wait_ge(s_split, n * 4 + 3)
                    nc.vector.tensor_sub(third, left, second).then_inc(s_split, 1)
                    dve.wait_ge(s_split, n * 4 + 4)

                def find_rows(k, n, slot):
                    dve.wait_ge(s_src[slot], k * 16 + 32)
                    of = src_i[:, slot, PICKED:PICKED + 1]
                    nc.vector.tensor_scalar(place_i[:, 0:1], of, P - 1, None, ALU.bitwise_and).then_inc(s_place, 1)
                    nc.vector.tensor_scalar(place_i[:, 1:2], of, P.bit_length() - 1, None,
                                            ALU.logical_shift_right).then_inc(s_place, 1)
                    dve.wait_ge(s_place, n * 3 + 2)
                    nc.vector.tensor_copy(place[:, :], place_i[:, :]).then_inc(s_place, 1)
                    dve.wait_ge(s_place, n * 3 + 3)
                    nc.vector.memset(kept[:, :, :], 0.0)
                    for to, i in ((hot_row, 0), (hot_tile, 1)):
                        m = to.shape[1]
                        nc.vector.tensor_tensor(to[:, :], iota[:, 0:m], place[:, i:i + 1].to_broadcast([P, m]),
                                                ALU.is_equal).then_inc(s_hot, 1)

                def copy_rows_T(n):
                    dve.wait_ge(s_hotT, n + 1)
                    nc.vector.tensor_copy(rows_T[:, :], pick_ps[1][:, 0:P]).then_inc(s_rowsT, 1)

                def pick(n, r, slot):
                    m = min(HB, NT - r * HB)
                    dve.wait_ge(s_round, n * ROUNDS + r + 1)
                    if r:
                        dve.wait_ge(s_picked, n * ROUNDS + r)
                    dve.nop(nofuse=True)
                    nc.vector.copy_predicated(
                        kept[:, 0:m, :],
                        hot_tile[:, r * HB:r * HB + m].unsqueeze(2).to_broadcast([P, m, H]),
                        pick_ps[r % 2][:, 0:m * H].rearrange("p (k f) -> p k f", f=H)).then_inc(s_picked, 1)
                    if r == ROUNDS - 1:
                        dve.wait_ge(s_picked, n * ROUNDS + ROUNDS)
                        nc.vector.tensor_reduce(edge_in[:, slot, PICKED, XS], kept[:, :, :].rearrange("p k f -> p f k"),
                                                AX.X, ALU.add).then_inc(s_row, 1)

                def groups(k, j=None):
                    for u in range(S):
                        half, h = divmod(u, HS)

                        def picks(*places):
                            if j is not None:
                                for r in (r for place in places for r in BESIDE[h][place]):
                                    pick(j * 2 + half, r, half * HS)

                        copy_inputs(k * S + (u + 1))
                        if j is None:
                            split(k * S + u, (k * S + u) * SPLIT, SPLIT)
                        elif h == 0:
                            find_rows(k, j * 2 + half, half * HS)
                        picks(AFTER_INPUTS)
                        prepare(k * S + (u + 2), (u + 2) % S, k * 16 + 16 * ((u + 2) // S + 1))
                        if j is not None and h == 0:
                            copy_rows_T(j * 2 + half)
                        picks(AFTER_SECOND, AFTER_FIRST)
                        add_messages(k * S + u, lambda: picks(AFTER_EDGES))
                        picks(AFTER_SUMS)

                with dve.Fori(0, ITERS) as k:
                    groups(k)
                split(SPAN, SPAN * SPLIT, NT - SPAN * SPLIT)
                with dve.Fori(0, LOTS) as b:
                    with dve.Fori(0, ITERS) as i:
                        groups(b * ITERS + i + ITERS, b * ITERS + i)
                    with dve.If(late == 0):
                        inner_lot(b)
                for g in range(REST, NG):
                    copy_inputs(g)
                    if g < FULL:
                        tail = g + 1 == FULL
                        prepare(g + 1, (g + 1) % S, 16 * ((g + 1) // S + 1 + tail))
                    add_messages(g - 1)
                add_messages(FULL)
                dve.wait_ge(s_added, NG)
                nc.vector.memset(done_mark[:, :], 0.0).then_inc(s_sums, 1)
            with dve.Else():
                any_tiles = edge_in[:, ANY, :, :]

                def any_group(g, loaded, tiles):
                    if tiles < T:
                        dve.wait_ge(a_rel, FULL * (NT + 1))
                        nc.vector.memset(dst_rel[:, tiles:T], -1.0)
                    dve.wait_ge(a_load, loaded)
                    nc.vector.tensor_copy(dst_rel[:, 0:tiles], dst_i[:, 0, 0:tiles]).then_inc(a_rel, 1)
                    for ends in (SRC, DST):
                        dve.wait_ge(a_T, g * 2 + (ends + 1))
                        nc.vector.tensor_copy(in_T[:, 0, :], in_ps[0][:, :])
                        nc.vector.tensor_copy(in_T[:, 1, :], in_ps[1][:, :]).then_inc(a_Tc, 1)
                    dve.wait_ge(a_msg, g + 1)
                    nc.vector.tensor_copy(msg[:, :, :, :].rearrange("p c a f -> p (c a f)"),
                                          msg_ps[:, :]).then_inc(a_msgc, 1)
                    with dve.Fori(0, NT) as k:
                        dve.wait_ge(a_rel, g * (NT + 1) + k + 1)
                        nc.vector.tensor_tensor(
                            any_tiles, iota[:, :].unsqueeze(1).to_broadcast([P, T, P]),
                            dst_rel[:, :].unsqueeze(2).to_broadcast([P, T, P]), ALU.is_equal).then_inc(a_oh, 1)
                        dve.wait_ge(a_oh, g * NT + k + 1)
                        nc.vector.tensor_scalar(dst_rel[:, :], dst_rel[:, :], float(-P), None,
                                                ALU.add).then_inc(a_rel, 1)
                        dve.wait_ge(a_agg, g * NT + k + 1)
                        sums = node_T[H:P, bass.ds(k * P, P)]
                        nc.vector.tensor_add(sums, sums, agg_ps[H:P, 0:P]).then_inc(a_added, 1)

                for s in range(S):
                    dve.wait_ge(s_xg[s], 16 * T)
                nc.vector.memset(edge_in[:, SRC:DST + 1, :, :], 0.0).then_inc(a_clear, 1)
                with dve.Fori(0, FULL) as g:
                    any_group(g, g * 48 + 48, T)
                any_group(FULL, FULL * 48 + 48, TT)
                dve.wait_ge(a_added, NG * NT)
                nc.vector.memset(done_mark[:, :], 0.0).then_inc(s_sums, 1)

            with dve.If(late == 1):
                with dve.Fori(0, LOTS) as b:
                    inner_lot(b)
            update_lot(LOTS, LAST_T, xs[:, LOTS * LT:NT, :])

        @block.tensor
        def _(pe):
            pe.wait_ge(s_ident, 2)
            pe.wait_ge(s_chk, 2)
            nc.tensor.matmul(z1_ps[:, 0:Q * P], ones[:, :], base_diag[:, :, :].rearrange("p q c -> p (q c)"),
                             start=True, stop=True).then_inc(s_base, 1)
            pe.wait_ge(s_chk, 6)
            nc.tensor.transpose(z2_ps[0:2, 0:P], outside[:, :], ident[:, :]).then_inc(s_out_T, 1)

            pe.wait_ge(s_x, 16 * 2)
            for n, (a, b) in enumerate(xT_banks):
                if n >= 2:
                    pe.wait_ge((s_xT_a, s_xT_v)[n % 2], n // 2)
                for j, k in enumerate(range(a, b)):
                    last = nc.tensor.transpose(in_ps[n % 2][0:H, j * P:(j + 1) * P], xs[:, k, :], ident[:, :])
                last.then_inc(s_xT_ps, 1)
            pe.wait_ge(s_xT_a, -(-len(xT_banks) // 2))
            pe.wait_ge(s_xT_v, len(xT_banks) // 2)
            pe.wait_ge(s_w, 16 * n_weights)
            pe.wait_ge(s_flag, 1)

            def transpose_tiles(s):
                for t in range(T):
                    last = nc.tensor.transpose(in_ps[t // HT][:, t % HT * P:(t % HT + 1) * P],
                                               edge_in[:, s, t, :], ident[:, :])
                return last

            def transpose_inputs(g, s, gathered):
                pe.wait_ge(s_xwin, g + 1)
                pe.wait_ge(s_oh, g + 1)
                pe.wait_ge(s_eac, g + 1)
                pe.wait_ge(s_xg[s], gathered)
                transpose_tiles(s).then_inc(s_in_T, 1)
                nc.tensor.matmul(agg_ps[OH, 0:H], xwin[:, :], w1b[:, :], start=True, stop=True).then_inc(s_bwin, 1)

            def first_layer(g):
                pe.wait_ge(s_bwc, g + 1)
                pe.wait_ge(s_in1c, g + 1)
                nc.tensor.matmul(z1_ps[0:H, :], w_in[:, :], in_T[:, 0, :], start=True, stop=True)
                nc.tensor.matmul(z1_ps[H:P, :], w_in[:, :], in_T[:, 1, :], start=True, stop=True).then_inc(s_z1, 1)

            def second_layer(g):
                pe.wait_ge(s_h, g + 1)
                nc.tensor.matmul(z2_ps[:, :], w2_bd[:, :], h_T[:, :], start=True, stop=True).then_inc(s_z2, 1)

            def by_edges():
                for c in range(HT):
                    last = nc.tensor.transpose(msg_ps[:, c * P:(c + 1) * P], msg_T[:, c * P:(c + 1) * P], ident[:, :])
                return last

            def sum_by_node(s, nodes):
                for t in range(T):
                    last = nc.tensor.matmul(agg_ps[H:P, nodes], msg[:, t % HT, t // HT, :], edge_in[:, s, t, nodes],
                                            start=(t == 0), stop=(t == T - 1))
                return last

            def sum_messages(g, s, beside=None):
                pe.wait_ge(s_msgT, g + 1)
                by_edges().then_inc(s_msg, 1)
                if beside:
                    beside()
                pe.wait_ge(s_msgc, g + 1)
                sum_by_node(s, OH).then_inc(s_agg, 1)

            def update_lot(b, m, lot):
                half = m * P // 2
                for a in range(2):
                    last = nc.tensor.matmul(z2_ps[a * H:(a + 1) * H, 0:half], w3[:, :], lot[:, a * half:(a + 1) * half],
                                            start=True, stop=True)
                last.then_inc(s_z3, 1)
                pe.wait_ge(s_upd, b + 1)
                for c in range(m // 2):
                    last = nc.tensor.transpose(upd_ps[:, c * P:(c + 1) * P], upd_T[:, c * P:(c + 1) * P], ident[:, :])
                last.then_inc(s_updT, 1)

            def inner_lot(b):
                pe.wait_ge(s_lot, b + 1)
                update_lot(b, LT, lot_T)

            general = pe.value_load(flags_i[0:1, 0:1], min_val=0, max_val=1)
            late = pe.value_load(flags_i[1:2, 0:1], min_val=0, max_val=1)
            with pe.If(general == 0):
                transpose_inputs(0, 0, 16 * T)
                first_layer(0)
                def transpose_hot_row(n):
                    pe.wait_ge(s_hot, n * 2 + 2)
                    nc.tensor.transpose(pick_ps[1][:, 0:P], hot_row[:, :], ident[:, :]).then_inc(s_hotT, 1)

                def pick_round(n, r):
                    m = min(HB, NT - r * HB)
                    if r == 0:
                        pe.wait_ge(s_rowsT, n + 1)
                    elif r >= 2:
                        pe.wait_ge(s_picked, n * ROUNDS + r - 1)
                    for i in range(PARTS):
                        last = nc.tensor.matmul(pick_ps[r % 2][:, 0:m * H], rows_T[:, :],
                                                parts[:, i, r * HB:r * HB + m, :].rearrange("p k f -> p (k f)"),
                                                start=(i == 0), stop=(i == PARTS - 1))
                    last.then_inc(s_round, 1)

                def groups(k, j=None):
                    for u in range(S):
                        g, s, uses = k * S + (u + 1), (u + 1) % S, (u + 1) // S + 1
                        half, h = divmod(u, HS)

                        def rounds(place):
                            if j is not None:
                                for r in BESIDE[h][place]:
                                    pick_round(j * 2 + half, r)

                        gathered = k * (16 * T) + 16 * T * uses
                        if j is not None and s == 0:
                            pe.wait_ge(s_row, j * 2 + 1)
                            gathered = j * (16 * PICKED) + 16 * (T * FIRST + PICKED)
                        elif j is not None and s == HS:
                            gathered = j * (16 * PICKED) + 16 * T * FIRST
                        transpose_inputs(g, s, gathered)
                        rounds(AFTER_INPUTS)
                        second_layer(k * S + u)
                        rounds(AFTER_SECOND)
                        first_layer(g)
                        if j is not None and h == 0:
                            transpose_hot_row(j * 2 + half)
                        rounds(AFTER_FIRST)
                        sum_messages(k * S + u, u, lambda: rounds(AFTER_EDGES))
                        rounds(AFTER_SUMS)

                with pe.Fori(0, ITERS) as k:
                    groups(k)
                with pe.Fori(0, LOTS) as b:
                    with pe.Fori(0, ITERS) as i:
                        groups(b * ITERS + i + ITERS, b * ITERS + i)
                    with pe.If(late == 0):
                        inner_lot(b)
                for g in range(REST, NG):
                    gathered = T * (g // S + 1)
                    if g % HS == 0:
                        pe.wait_ge(s_row, 2 * (FULL // S - FIRST))
                        gathered = T * FIRST + PICKED * (FULL // S - FIRST) + (TT if g == FULL else 0)
                    transpose_inputs(g, g % S, 16 * gathered)
                    second_layer(g - 1)
                    first_layer(g)
                    sum_messages(g - 1, (g - 1) % S)
                second_layer(FULL)
                sum_messages(FULL, FULL % S)
            with pe.Else():
                def any_group(g, gathered):
                    pe.wait_ge(a_eac, g + 1)
                    for ends, w in ((SRC, w_in), (DST, w_dst)):
                        pe.wait_ge(a_gath[ends], gathered)
                        transpose_tiles(ends).then_inc(a_T, 1)
                        pe.wait_ge(a_Tc, g * 2 + (ends + 1))
                        for half in range(2):
                            last = nc.tensor.matmul(z1_ps[half * H:(half + 1) * H, :], w[:, :], in_T[:, half, :],
                                                    start=(ends == SRC), stop=(ends == DST))
                    last.then_inc(a_z1, 1)
                    pe.wait_ge(a_h, g + 1)
                    nc.tensor.matmul(z2_ps[:, :], w2_bd[:, :], h_T[:, :], start=True, stop=True).then_inc(a_z2, 1)
                    pe.wait_ge(a_msgT, g + 1)
                    by_edges().then_inc(a_msg, 1)
                    pe.wait_ge(a_msgc, g + 1)
                    pe.nop(nofuse=True)
                    with pe.Fori(0, NT) as k:
                        pe.wait_ge(a_oh, g * NT + k + 1)
                        sum_by_node(ANY, slice(0, P)).then_inc(a_agg, 1)

                with pe.Fori(0, FULL) as g:
                    any_group(g, g * (16 * T) + 16 * T)
                any_group(FULL, 16 * (T * FULL + TT))

            with pe.If(late == 1):
                with pe.Fori(0, LOTS) as b:
                    inner_lot(b)
            pe.wait_ge(s_sums, 1)
            pe.wait_ge(s_res, LOTS)
            update_lot(LOTS, LAST_T, node_T[:, LOTS * LN:NPAD])


_INS = ["x", "src", "dst", "edge_attr_16", "L0_gnn_W1", "L0_gnn_b1", "L0_gnn_W2", "L0_gnn_b2", "L0_gnn_W3", "L0_gnn_b3"]


def kernel(**inputs):
    import numpy as _np
    import concourse.bacc as _bacc
    from concourse import mybir as _mybir
    from concourse.bass_utils import run_bass_kernel_spmd as _run

    nc = _bacc.Bacc("TRN2", target_bir_lowering=False, num_devices=1)
    arrays, args = {}, []
    for name in _INS:
        a = _np.ascontiguousarray(inputs[name])
        arrays[f"in_{name}_dram"] = a
        args.append(nc.dram_tensor(f"in_{name}_dram", a.shape, _mybir.dt.from_np(a.dtype), kind="ExternalInput").ap())
    out = nc.dram_tensor("out_0_dram", inputs["x"].shape, _mybir.dt.float32, kind="ExternalOutput").ap()
    gnn_layer(nc, *args, out)
    r = _run(nc, [arrays], core_ids=[0])
    return r.results[0]["out_0_dram"]
```

```python
import concourse.bass as bass
import concourse.mybir as mybir
from contextlib import ExitStack


def gnn_layer(nc, x, src, dst, edge_attr, W1, b1, W2, b2, W3, b3, out):
    F32, I32, BF16 = mybir.dt.float32, mybir.dt.int32, mybir.dt.bfloat16
    ALU, ACT, AX = mybir.AluOpType, mybir.ActivationFunctionType, mybir.AxisListType

    P = 128
    N, H = x.shape
    E, D = edge_attr.shape
    T = 8
    HT = T // 2
    G = P * T
    FULL = E // G
    TT = (E - FULL * G) // P
    assert 0 < TT < T and E == FULL * G + TT * P and 2 * H == P and T * D == P
    NG = FULL + 1
    WIN = P - H - D
    LASTW = N - WIN
    OH, XS, EA = slice(0, WIN), slice(WIN, WIN + H), slice(WIN + H, P)
    NT = -(-N // P)
    NPAD = NT * P
    N0 = (NT - 1) * P
    NREM = N - N0
    S = 6
    B = 2 * S
    TURNS = B // S
    BODIES = (FULL - 1) // B
    assert FULL % S == 0 and FULL - S == BODIES * B
    REST = FULL - S + 1
    QF = FULL // P
    QR = FULL - QF * P
    Q = QF + 1
    EPS = 1e-5
    C = HT * P
    NB = 4
    ITERS = 2
    SPAN = ITERS * B
    SEGS = BODIES // ITERS
    LAG = 4
    LT = SPAN * G * N // (E * P)
    LN = LT * P
    LOTS = SEGS - 1
    LAST_T = NT - LOTS * LT
    assert SEGS * ITERS == BODIES and LN % SPAN == 0 and LT % 2 == 0 and LAST_T == T and LT < T
    BESIDE_GROUPS = [3, 3, 2, 2, 2]
    NPICK = len(BESIDE_GROUPS)
    MADE = [(p, h) for p, many in enumerate(BESIDE_GROUPS) for h in range(many)]
    PICKED_AT = [MADE.index((p, 0)) % B for p in range(NPICK)]
    PICKED = T - 1
    FIRST = ITERS * TURNS + 1
    assert len(MADE) == B and TURNS == 2
    PARTS = 3
    SPLIT = NT // SPAN
    HB = C // H
    ROUNDS = 2
    PLACES = ROUNDS * HB
    SETS = -(-NT // PLACES)
    ROW_BITS, PLACE_BITS = P.bit_length() - 1, PLACES.bit_length() - 1
    PIECES = [(r, c) for r in range(ROUNDS) for c in range(SETS) if c * PLACES + r * HB < NT]
    AFTER_INPUTS, AFTER_SECOND, AFTER_FIRST, AFTER_SUMS = range(4)
    BESIDE = {3: [(0, 0, 0, 0), (0, 0, 3, 3), (2, 2, 3, 0)], 2: [(0, 0, 0, 0), (0, 0, 13, 0)]}
    for many in BESIDE_GROUPS:
        assert sum(sum(n) for n in BESIDE[many]) == len(PIECES)
    assert P == 1 << ROW_BITS and PLACES == 1 << PLACE_BITS
    assert all(b[-1][AFTER_SUMS] == 0 for b in BESIDE.values())
    SRC, DST, ANY = 0, 1, 2

    ctx = ExitStack()
    with ctx:
        def sb(name, shape, dt=F32):
            return ctx.enter_context(nc.sbuf_tensor(name, shape, dt))

        def pb(name):
            return ctx.enter_context(nc.psum_tensor(name, [P, C], F32))

        def sem(name):
            return ctx.enter_context(nc.semaphore(name))

        node_T = sb("node_T", [P, NPAD])
        xs = sb("xs", [P, NT, H])
        ident = sb("ident", [P, P])
        iota = sb("iota", [P, P])
        ones = sb("ones", [P, P])
        zero_col = sb("zero_col", [P, 1])
        w_in = sb("w_in", [P, H])
        w_dst = sb("w_dst", [P, H])
        w1b = sb("w1b", [H, H])
        w2_bd = sb("w2_bd", [P, P])
        w3 = sb("w3", [P, H])
        b1_col = sb("b1_col", [P, 1])
        b2_rep = sb("b2_rep", [P, H])
        b3_col = sb("b3_col", [P, 1])
        base_bc = sb("base_bc", [P, Q * P])
        base_i = sb("base_i", [1, Q * P], I32)
        no_node = sb("no_node", [P, T], I32)
        dst_g = sb("dst_g", [P, Q, G], I32)
        hi = sb("hi", [P, Q])
        lo = sb("lo", [P, Q])
        base_g = sb("base_g", [P, Q])
        base_diag = sb("base_diag", [P, Q, P])
        early = sb("early", [P, Q])
        outside = sb("outside", [P, 2])
        outside_all = sb("outside_all", [2, 1])
        flags_i = sb("flags_i", [2, 1], I32)
        parts = sb("parts", [P, PARTS, NT, H], BF16)
        rest = sb("rest", [P, SPLIT, H])
        iota_sets = sb("iota_sets", [P, SETS, P])
        place_i = sb("place_i", [P, 3], I32)
        place = sb("place", [P, 3])
        set_row = sb("set_row", [P, 1])
        hot_row = sb("hot_row", [P, SETS, P])
        hot_place = [sb("hot_place0", [P, HB]), sb("hot_place1", [P, HB], I32)]
        kept = sb("kept", [P, HB, H])
        rows_T = sb("rows_T", [P, SETS, P], BF16)
        src_i = sb("src_i", [P, S, T], I32)
        dst_i = sb("dst_i", [P, S, T], I32)
        ea = sb("ea", [P, S, T, D])
        edge_in = sb("edge_in", [P, S, T, P])
        dst_rel = sb("dst_rel", [P, T])
        xwin = sb("xwin", [H, WIN])
        in_T = sb("in_T", [P, 2, C])
        h_T = sb("h_T", [P, C])
        msg = sb("msg", [P, HT, 2, H])
        lot_T = sb("lot_T", [P, LN])
        upd_T = sb("upd_T", [P, C])
        y = sb("y", [P, T, H])
        square = sb("square", [P, T, H])
        result = sb("result", [P, T, H])
        total = sb("total", [P, T])
        var = sb("var", [P, T])
        rstd = sb("rstd", [P, T])
        tables = sb("tables", [P, 1])
        done_mark = sb("done_mark", [1, 1])

        in_ps = [pb("in_ps0"), pb("in_ps1")]
        z1_ps = pb("z1_ps")
        z2_ps = pb("z2_ps")
        agg_ps = pb("agg_ps")
        pick_ps = [pb("pick_ps0"), pb("pick_ps1")]
        upd_ps = pb("upd_ps")

        s_zeroed = sem("zeroed")
        s_ident = sem("ident_made")
        s_const = sem("iota_made")
        s_dst_g = sem("dst_g_loaded")
        s_x = sem("x_loaded")
        s_w = sem("weights_loaded")
        s_chk = sem("check_step")
        s_base = sem("base_spread")
        s_out_T = sem("outside_transposed")
        s_flag = sem("general_known")
        s_sum0 = sem("sums_cleared")
        s_xT_ps = sem("x_transposed")
        s_xT_a = sem("x_T_copied_act")
        s_xT_v = sem("x_T_copied_dve")
        s_src = [sem(f"src_loaded{s}") for s in range(S)]
        s_dst = [sem(f"dst_loaded{s}") for s in range(S)]
        s_ea = [sem(f"ea_loaded{s}") for s in range(S)]
        s_xg = [sem(f"x_gathered{s}") for s in range(S)]
        s_eac = sem("ea_placed")
        s_xwin = sem("window_copied")
        s_rel = sem("dst_rel_made")
        s_oh = sem("onehot_made")
        s_in_T = sem("edge_in_transposed")
        s_bwin = sem("window_projected")
        s_in0c = sem("first_half_copied")
        s_in1c = sem("second_half_copied")
        s_bwc = sem("window_placed")
        s_z1 = sem("z1_done")
        s_h = sem("h_done")
        s_z2 = sem("z2_done")
        s_biased = sem("z2_biased")
        s_msg = sem("messages_done")
        s_agg = sem("window_summed")
        s_added = sem("window_added")
        s_split = sem("split_step")
        s_iota = sem("iota_sets_made")
        s_place = sem("src_placed")
        s_hot = sem("hot_made")
        s_hotT = sem("hot_row_transposed")
        s_rowsT = sem("rows_T_made")
        s_round = sem("round_done")
        s_picked = sem("rows_picked")
        s_row = sem("picked_tile_made")
        a_clear = sem("any_cleared")
        a_load = sem("any_loaded")
        a_gath = [sem("any_x_src_gathered"), sem("any_x_dst_gathered")]
        a_eac = sem("any_ea_placed")
        a_rel = sem("any_dst_rel_made")
        a_T = sem("any_edge_in_transposed")
        a_Tc = sem("any_edge_in_copied")
        a_z1 = sem("any_z1_done")
        a_h = sem("any_h_done")
        a_z2 = sem("any_z2_done")
        a_biased = sem("any_z2_biased")
        a_msg = sem("any_messages_done")
        a_oh = sem("any_onehot_made")
        a_agg = sem("any_tile_summed")
        a_added = sem("any_tile_added")
        s_sums = sem("sums_complete")
        s_lot = sem("lot_copied")
        s_z3 = sem("z3_done")
        s_upd = sem("update_done")
        s_updT = sem("update_transposed")
        s_res = sem("residual_added")
        s_tot = sem("features_summed")
        s_cen = sem("centred")
        s_sq = sem("squared")
        s_sqr = sem("squares_summed")
        s_var = sem("variance_done")
        s_std = sem("std_done")
        s_rstd = sem("rstd_done")
        s_norm = sem("normalised")
        s_out = sem("out_stored")

        block = ctx.enter_context(nc.Block())

        src_v = src[0:FULL * G].rearrange("(g p t) -> g p t", p=P, t=T)
        dst_v = dst[0:FULL * G].rearrange("(g p t) -> g p t", p=P, t=T)
        ea_v = edge_attr[0:FULL * G, :].rearrange("(g p t) d -> g p t d", p=P, t=T)
        src_tail = src[FULL * G:E].rearrange("(p t) -> p t", t=TT)
        dst_tail = dst[FULL * G:E].rearrange("(p t) -> p t", t=TT)
        ea_tail = edge_attr[FULL * G:E, :].rearrange("(p t) d -> p t d", t=TT)
        PICKED_SLOTS = [[at - turn * S for at in PICKED_AT if at // S == turn] for turn in range(TURNS)]
        n_weights = 5 + 2 + 1 + 4
        xT_banks = [(k, min(k + NB, NT)) for k in range(0, NT, NB)]

        def row(w):
            return w.rearrange("(a n) -> a n", a=1)

        msg_all = msg[:, :, :, :].rearrange("p c a f -> p (c a f)")

        def column(w):
            return w.rearrange("(n a) -> n a", a=1)

        def halves(m, psum):
            if psum:
                return upd_ps[:, 0:m * H].rearrange("p (c a f) -> p a c f", a=2, f=H)
            return y[:, 0:m, :].rearrange("p (a c) f -> p a c f", a=2)

        @block.sync
        def _(sp):
            def load_rest(n, g, s):
                sp.dma_start(dst_i[:, s, :], dst_v[g]).then_inc(s_dst[s], 16)
                sp.dma_start(ea[:, s, :, :], ea_v[g]).then_inc(s_ea[s], 16)

            for g in range(S):
                sp.dma_start(src_i[:, g, :], src_v[g]).then_inc(s_src[g], 16)
            sp.dma_start(dst_g[:, 0:QF, :],
                         dst[0:QF * P * G].rearrange("(q p e) -> p q e", p=P, e=G)).then_inc(s_dst_g, 16)
            sp.wait_ge(s_zeroed, 1)
            sp.dma_start(dst_g[0:QR, QF, :],
                         dst[QF * P * G:FULL * G].rearrange("(p e) -> p e", e=G)).then_inc(s_dst_g, 16)
            sp.dma_start(dst_g[QR:QR + 1, QF, 0:TT * P], row(dst[FULL * G:E])).then_inc(s_dst_g, 16)
            sp.dma_start(dst_g[QR:QR + 1, QF, TT * P:G],
                         row(dst[FULL * G:FULL * G + G - TT * P])).then_inc(s_dst_g, 16)
            sp.dma_start(xs[:, 0:NT - 1, :],
                         x[0:N0, :].rearrange("(k p) f -> p k f", p=P)).then_inc(s_x, 16)
            sp.wait_ge(s_zeroed, 2)
            sp.dma_start(xs[0:NREM, NT - 1, :], x[N0:N, :]).then_inc(s_x, 16)
            sp.wait_ge(s_flag, 1)
            general = sp.value_load(flags_i[0:1, 0:1], min_val=0, max_val=1)
            with sp.If(general == 0):
                for g in range(S):
                    load_rest(0, g, g)
                with sp.Fori(1, FULL // S) as k:
                    for s in range(S):
                        sp.wait_ge(s_rel, k * S + (s - S + 1))
                        sp.wait_ge(s_in_T, k * S + (s - S + 1))
                        sp.nop(nofuse=True)
                        sp.dma_start(src_i[:, s, :], src_v[k * S + s]).then_inc(s_src[s], 16)
                        load_rest(k, k * S + s, s)
                sp.wait_ge(s_rel, FULL - S + 1)
                sp.wait_ge(s_in_T, FULL - S + 1)
                sp.dma_start(src_i[:, 0, 0:TT], src_tail).then_inc(s_src[0], 16)
                sp.dma_start(dst_i[:, 0, 0:TT], dst_tail).then_inc(s_dst[0], 16)
                sp.dma_start(dst_i[:, 0, TT:T], no_node[:, TT:T]).then_inc(s_dst[0], 16)
                sp.dma_start(ea[:, 0, 0:TT, :], ea_tail).then_inc(s_ea[0], 16)
            with sp.Else():
                sp.wait_ge(a_clear, 1)

                def load_any(g):
                    sp.dma_start(src_i[:, 0, :], src_v[g]).then_inc(a_load, 16)
                    sp.dma_start(dst_i[:, 0, :], dst_v[g]).then_inc(a_load, 16)
                    sp.dma_start(ea[:, 0, :, :], ea_v[g]).then_inc(a_load, 16)

                load_any(0)
                with sp.Fori(1, FULL) as g:
                    sp.wait_ge(a_added, g * NT)
                    sp.nop(nofuse=True)
                    load_any(g)
                sp.wait_ge(a_added, FULL * NT)
                sp.dma_start(src_i[:, 0, 0:TT], src_tail).then_inc(a_load, 16)
                sp.dma_start(dst_i[:, 0, 0:TT], dst_tail).then_inc(a_load, 16)
                sp.dma_start(ea[:, 0, 0:TT, :], ea_tail).then_inc(a_load, 16)
            sp.wait_ge(s_out, 16 * (LOTS + 3))

        @block.gpsimd
        def _(pool):
            nc.gpsimd.memset(ident[:], 0.0).then_inc(s_ident, 1)
            pool.wait_ge(s_ident, 1)
            nc.gpsimd.affine_select(out=ident[:], in_=ident[:], compare_op=ALU.not_equal, fill=1.0, base=0,
                                    pattern=[[-1, P]], channel_multiplier=1).then_inc(s_ident, 1)
            nc.gpsimd.iota(iota[:], pattern=[[1, P]], base=0, channel_multiplier=0,
                           allow_small_or_imprecise_dtypes=True).then_inc(s_const, 1)
            nc.gpsimd.iota(early[:], pattern=[[P * (LN // SPAN), Q]], base=LN // SPAN * LAG - LN, channel_multiplier=LN // SPAN,
                           allow_small_or_imprecise_dtypes=True).then_inc(s_const, 1)

            def gather(indices, from_slot, to_slot, tiles, arrived):
                for t in range(tiles):
                    pool.indirect_dma_start(
                        out=edge_in[:, to_slot, t, XS], out_offset=None, in_=x[:, :],
                        in_offset=bass.IndirectOffsetOnAxis(ap=indices[:, from_slot, t:t + 1], axis=0),
                    ).then_inc(arrived, 16)

            for s in range(S):
                pool.wait_ge(s_src[s], 16)
                gather(src_i, s, s, T, s_xg[s])
            pool.wait_ge(s_flag, 1)
            general = pool.value_load(flags_i[0:1, 0:1], min_val=0, max_val=1)
            with pool.If(general == 0):
                def fill_slots(k, picked=()):
                    for s in range(S):
                        pool.wait_ge(s_in_T, k * S + (s - S + 1))
                        pool.wait_ge(s_src[s], k * 16 + 16)
                        pool.nop(nofuse=True)
                        gather(src_i, s, s, PICKED if s in picked else T, s_xg[s])

                with pool.Fori(1, FIRST) as k:
                    fill_slots(k)
                with pool.Fori(0, BODIES - ITERS) as j:
                    for turn in range(TURNS):
                        fill_slots(j * TURNS + (FIRST + turn), PICKED_SLOTS[turn])
                pool.wait_ge(s_in_T, FULL - S + 1)
                pool.wait_ge(s_src[0], 16 * (FULL // S + 1))
                gather(src_i, 0, 0, TT, s_xg[0])
            with pool.Else():
                def gather_both(tiles):
                    gather(src_i, 0, SRC, tiles, a_gath[SRC])
                    gather(dst_i, 0, DST, tiles, a_gath[DST])

                with pool.Fori(0, FULL) as g:
                    pool.wait_ge(a_load, g * 48 + 48)
                    pool.nop(nofuse=True)
                    gather_both(T)
                pool.wait_ge(a_load, FULL * 48 + 48)
                gather_both(TT)

        @block.scalar
        def _(act):
            act.wait_ge(s_zeroed, 2)
            loads = [(w_in[XS, :], W1[0:H, :]), (w_in[EA, :], W1[2 * H:2 * H + D, :]),
                     (w_dst[XS, :], W1[H:2 * H, :]), (w1b[:, :], W1[H:2 * H, :]), (w3[:, :], W3),
                     (w2_bd[0:H, 0:H], W2), (w2_bd[H:P, H:P], W2)]
            loads += [(b2_rep[:, :], row(b2).to_broadcast([P, H]))]
            for col, b in ((b1_col, b1), (b3_col, b3)):
                loads += [(col[0:H, :], column(b)), (col[H:P, :], column(b))]
            for to, of in loads:
                act.dma_start(to, of).then_inc(s_w, 16)
            nc.scalar.copy(node_T[H:P, :], zero_col[H:P, :].to_broadcast([H, NPAD])).then_inc(s_sum0, 1)

            for n in range(0, len(xT_banks), 2):
                a, b = xT_banks[n]
                act.wait_ge(s_xT_ps, n + 1)
                nc.scalar.copy(node_T[0:H, a * P:b * P], in_ps[0][0:H, 0:(b - a) * P]).then_inc(s_xT_a, 1)

            def place_ea(s, arrived):
                act.wait_ge(s_ea[s], arrived)
                nc.scalar.copy(edge_in[:, s, :, EA], ea[:, s, :, :]).then_inc(s_eac, 1)

            def copy_second_half(g):
                act.wait_ge(s_in_T, g + 1)
                nc.scalar.copy(in_T[:, 1, :], in_ps[1][:, :]).then_inc(s_in1c, 1)

            def first_silu(g):
                act.wait_ge(s_z1, g + 1)
                nc.scalar.activation(h_T[:, :], z1_ps[:, :], ACT.Silu, bias=b1_col[:, :]).then_inc(s_h, 1)

            def second_silu(g):
                act.wait_ge(s_biased, g + 1)
                nc.scalar.activation(msg_all, msg_all, ACT.Silu, bias=zero_col[:, :]).then_inc(s_msg, 1)

            act.wait_ge(s_w, 16 * n_weights)
            act.wait_ge(s_flag, 1)
            general = act.value_load(flags_i[0:1, 0:1], min_val=0, max_val=1)
            late = act.value_load(flags_i[1:2, 0:1], min_val=0, max_val=1)

            def update_lot(b, m, store):
                act.wait_ge(s_z3, b + 1)
                nc.scalar.activation(upd_T[:, 0:m * H], z2_ps[:, 0:m * H], ACT.Silu, bias=b3_col[:, :]).then_inc(s_upd, 1)
                act.wait_ge(s_var, b + 1)
                nc.scalar.activation(rstd[:, 0:m], var[:, 0:m], ACT.Sqrt).then_inc(s_std, 1)
                nc.scalar.activation(tables[:, :], zero_col[:, :], ACT.Silu, bias=zero_col[:, :])
                act.wait_ge(s_norm, b + 1)
                act.nop(nofuse=True)
                store()

            def inner_lot(b):
                nc.scalar.copy(lot_T[:, :], node_T[:, bass.ds(b * LN, LN)]).then_inc(s_lot, 1)
                update_lot(b, LT, lambda: act.dma_start(
                    out[bass.ds(b * LN, LN), :].rearrange("(k p) f -> p k f", p=P), result[:, 0:LT, :]).then_inc(s_out, 16))

            def last_lot():
                a = LOTS * LT
                act.dma_start(out[a * P:N0, :].rearrange("(k p) f -> p k f", p=P),
                              result[:, 0:NT - 1 - a, :]).then_inc(s_out, 16)
                act.dma_start(out[N0:N, :], result[0:NREM, NT - 1 - a, :]).then_inc(s_out, 16)

            with act.If(general == 0):
                place_ea(0, 16)
                copy_second_half(0)
                first_silu(0)
                place_ea(1, 16)

                def copy_rows_T(n):
                    act.wait_ge(s_hotT, n + 1)
                    for i in range(2):
                        a, b = i * HT, min(SETS, i * HT + HT)
                        nc.scalar.copy(rows_T[:, a:b, :].rearrange("p c e -> p (c e)"),
                                       pick_ps[i][:, 0:(b - a) * P]).then_inc(s_rowsT, 1)

                def groups(k, j=None):
                    for u in range(B):
                        p, h = MADE[u]
                        copy_second_half(k * B + (u + 1))
                        place_ea((u + 2) % S, k * (16 * TURNS) + 16 * ((u + 2) // S + 1))
                        if j is not None and h == 1:
                            copy_rows_T(j * NPICK + p)
                        second_silu(k * B + u)
                        first_silu(k * B + (u + 1))

                with act.Fori(0, ITERS) as k:
                    groups(k)
                with act.Fori(0, LOTS) as b:
                    with act.Fori(0, ITERS) as i:
                        groups(b * ITERS + i + ITERS, b * ITERS + i)
                    with act.If(late == 0):
                        act.wait_ge(s_added, b * SPAN + (2 * SPAN - LAG))
                        inner_lot(b)
                for g in range(REST, NG):
                    copy_second_half(g)
                    second_silu(g - 1)
                    first_silu(g)
                    if g < FULL:
                        place_ea((g + 1) % S, 16 * ((g + 1) // S + 1))
                second_silu(FULL)
            with act.Else():
                def any_group(g, loaded, tiles):
                    act.wait_ge(a_load, loaded)
                    nc.scalar.copy(edge_in[:, SRC, 0:tiles, EA], ea[:, 0, 0:tiles, :]).then_inc(a_eac, 1)
                    act.wait_ge(a_z1, g + 1)
                    nc.scalar.activation(h_T[:, :], z1_ps[:, :], ACT.Silu, bias=b1_col[:, :]).then_inc(a_h, 1)
                    act.wait_ge(a_biased, g + 1)
                    nc.scalar.activation(msg_all, msg_all, ACT.Silu, bias=zero_col[:, :]).then_inc(a_msg, 1)

                act.wait_ge(a_clear, 1)
                with act.Fori(0, FULL) as g:
                    any_group(g, g * 48 + 48, T)
                any_group(FULL, FULL * 48 + 48, TT)

            with act.If(late == 1):
                act.wait_ge(s_sums, 1)
                with act.Fori(0, LOTS) as b:
                    inner_lot(b)
            update_lot(LOTS, LAST_T, last_lot)

        @block.vector
        def _(dve):
            steps = [0]

            def step(ins):
                ins.then_inc(s_chk, 1)
                steps[0] += 1
                dve.wait_ge(s_chk, steps[0])

            nc.vector.memset(dst_g[:, QF, :], N - 1).then_inc(s_zeroed, 1)
            nc.vector.memset(w_dst[:, :], 0.0)
            nc.vector.memset(w_in[OH, :], 0.0)
            nc.vector.memset(w2_bd[:, :], 0.0)
            nc.vector.memset(zero_col[:, :], 0.0)
            nc.vector.memset(no_node[:, :], -1)
            nc.vector.memset(result[:, :, :], 0.0).then_inc(s_out, 16)
            nc.vector.memset(ones[:, :], 1.0)
            nc.vector.memset(xs[:, NT - 1, :], 0.0).then_inc(s_zeroed, 1)

            dve.wait_ge(s_const, 1)
            for c in range(SETS):
                nc.vector.tensor_scalar(iota_sets[:, c, :], iota[:, :], float(c * P), None, ALU.add).then_inc(s_iota, 1)

            dve.wait_ge(s_dst_g, 4 * 16)
            nc.vector.tensor_reduce(hi[:, :], dst_g[:, :, :], AX.X, ALU.max)
            nc.vector.tensor_reduce(lo[:, :], dst_g[:, :, :], AX.X, ALU.min)
            step(nc.vector.tensor_scalar(base_g[:, :], dst_g[:, :, 0], float(LASTW), None, ALU.min))
            dve.wait_ge(s_ident, 2)
            for q in range(Q):
                last = nc.vector.tensor_scalar(base_diag[:, q, :], ident[:, :], base_g[:, q:q + 1], None, ALU.mult)
            step(last)
            dve.wait_ge(s_const, 2)
            nc.vector.tensor_sub(hi[:, :], hi[:, :], base_g[:, :])
            nc.vector.tensor_scalar(early[:, :], early[:, :], float(LN // SPAN * (FULL + LAG) - LN), None, ALU.min)
            step(nc.vector.tensor_sub(lo[:, :], base_g[:, :], lo[:, :]))
            nc.vector.tensor_sub(early[:, :], early[:, :], base_g[:, :])
            step(nc.vector.scalar_tensor_tensor(out=hi[:, :], in0=hi[:, :], scalar=float(1 - WIN), in1=lo[:, :],
                                                op0=ALU.add, op1=ALU.max))
            nc.vector.tensor_reduce(outside[:, 0:1], hi[:, :], AX.X, ALU.max)
            step(nc.vector.tensor_tensor(early[:, :], early[:, :], hi[:, :], ALU.max))
            step(nc.vector.tensor_reduce(outside[:, 1:2], early[:, :], AX.X, ALU.max))
            dve.wait_ge(s_out_T, 1)
            step(nc.vector.tensor_reduce(outside_all[:, :], z2_ps[0:2, 0:P], AX.X, ALU.max))
            nc.vector.tensor_scalar(flags_i[:, :], outside_all[:, :], 0.0, None, ALU.is_gt).then_inc(s_flag, 1)
            dve.wait_ge(s_base, 1)
            nc.vector.tensor_copy(base_bc[:, :], z1_ps[:, 0:Q * P])
            step(nc.vector.tensor_copy(base_i[:, :], z1_ps[0:1, 0:Q * P]))

            for n in range(1, len(xT_banks), 2):
                a, b = xT_banks[n]
                dve.wait_ge(s_xT_ps, n + 1)
                nc.vector.tensor_copy(node_T[0:H, a * P:b * P], in_ps[1][0:H, 0:(b - a) * P]).then_inc(s_xT_v, 1)

            def window_start(g):
                return dve.value_load(base_i[0:1, bass.ds(g, 1)], min_val=0, max_val=LASTW)

            def prepare(g, s, arrived):
                at = window_start(g)
                nc.vector.tensor_scalar(xwin[:, :], node_T[0:H, bass.ds(at, WIN)], 1.0, None,
                                        ALU.mult).then_inc(s_xwin, 1)
                dve.wait_ge(s_dst[s], arrived)
                nc.vector.tensor_scalar(dst_rel[:, :], dst_i[:, s, :], base_bc[:, bass.ds(g, 1)], None,
                                        ALU.subtract).then_inc(s_rel, 1)
                dve.wait_ge(s_rel, g + 1)
                nc.vector.tensor_tensor(
                    edge_in[:, s, :, OH], iota[:, OH].unsqueeze(1).to_broadcast([P, T, WIN]),
                    dst_rel[:, :].unsqueeze(2).to_broadcast([P, T, WIN]), ALU.is_equal).then_inc(s_oh, 1)

            def copy_inputs(g, first=False):
                if not first:
                    dve.wait_ge(s_z1, g)
                dve.wait_ge(s_in_T, g + 1)
                nc.vector.tensor_copy(in_T[:, 0, :], in_ps[0][:, :]).then_inc(s_in0c, 1)
                dve.wait_ge(s_bwin, g + 1)
                nc.vector.tensor_copy(w_in[OH, :], agg_ps[OH, 0:H]).then_inc(s_bwc, 1)

            def bias_z2():
                return nc.vector.tensor_add(msg[:, :, :, :].rearrange("p c a f -> p (c a) f"),
                                            z2_ps[:, :].rearrange("p (k f) -> p k f", f=H),
                                            b2_rep[:, :].unsqueeze(1).to_broadcast([P, T, H]))

            def add_bias(g):
                dve.wait_ge(s_z2, g + 1)
                bias_z2().then_inc(s_biased, 1)

            def add_messages(g):
                at = window_start(g)
                dve.wait_ge(s_agg, g + 1)
                sums = node_T[H:P, bass.ds(at, WIN)]
                nc.vector.tensor_add(sums, sums, agg_ps[H:P, OH]).then_inc(s_added, 1)

            dve.wait_ge(s_w, 16 * n_weights)
            dve.wait_ge(s_iota, SETS)
            dve.wait_ge(s_sum0, 1)
            dve.wait_ge(s_xT_a, -(-len(xT_banks) // 2))
            dve.wait_ge(s_xT_v, len(xT_banks) // 2)
            general = dve.value_load(flags_i[0:1, 0:1], min_val=0, max_val=1)
            late = dve.value_load(flags_i[1:2, 0:1], min_val=0, max_val=1)

            def update_lot(b, m, tiles):
                lot, rows = y[:, 0:m, :], total[:, 0:m]
                dve.wait_ge(s_updT, b + 1)
                nc.vector.tensor_add(halves(m, False), tiles.rearrange("p (a c) f -> p a c f", a=2),
                                     halves(m, True)).then_inc(s_res, 1)
                dve.wait_ge(s_res, b + 1)
                nc.vector.tensor_reduce(rows, lot, AX.X, ALU.add).then_inc(s_tot, 1)
                dve.wait_ge(s_tot, b + 1)
                nc.vector.scalar_tensor_tensor(out=lot, in0=rows.unsqueeze(2).to_broadcast([P, m, H]), scalar=-1.0 / H,
                                               in1=lot, op0=ALU.mult, op1=ALU.add).then_inc(s_cen, 1)
                dve.wait_ge(s_cen, b + 1)
                nc.vector.tensor_mul(square[:, 0:m, :], lot, lot).then_inc(s_sq, 1)
                dve.wait_ge(s_sq, b + 1)
                nc.vector.tensor_reduce(var[:, 0:m], square[:, 0:m, :], AX.X, ALU.add).then_inc(s_sqr, 1)
                dve.wait_ge(s_sqr, b + 1)
                nc.vector.tensor_scalar(var[:, 0:m], var[:, 0:m], 1.0 / H, EPS, ALU.mult, ALU.add).then_inc(s_var, 1)
                dve.wait_ge(s_std, b + 1)
                nc.vector.reciprocal(rstd[:, 0:m], rstd[:, 0:m]).then_inc(s_rstd, 1)
                dve.wait_ge(s_rstd, b + 1)
                dve.wait_ge(s_out, b * 16 + 16)
                nc.vector.tensor_mul(result[:, 0:m, :], lot,
                                     rstd[:, 0:m].unsqueeze(2).to_broadcast([P, m, H])).then_inc(s_norm, 1)

            def inner_lot(b):
                update_lot(b, LT, xs[:, bass.ds(b * LT, LT), :])

            with dve.If(general == 0):
                prepare(0, 0, 16)
                copy_inputs(0, first=True)
                prepare(1, 1, 16)

                def split(n, at, tiles):
                    of, left = xs[:, bass.ds(at, tiles), :], rest[:, 0:tiles, :]
                    first, second, third = (parts[:, i, bass.ds(at, tiles), :] for i in range(PARTS))
                    nc.vector.tensor_copy(first, of).then_inc(s_split, 1)
                    dve.wait_ge(s_split, n * 4 + 1)
                    nc.vector.tensor_sub(left, of, first).then_inc(s_split, 1)
                    dve.wait_ge(s_split, n * 4 + 2)
                    nc.vector.tensor_copy(second, left).then_inc(s_split, 1)
                    dve.wait_ge(s_split, n * 4 + 3)
                    nc.vector.tensor_sub(third, left, second).then_inc(s_split, 1)
                    dve.wait_ge(s_split, n * 4 + 4)

                def find_rows(n, slot, arrived):
                    dve.wait_ge(s_src[slot], arrived)
                    of = src_i[:, slot, PICKED:PICKED + 1]
                    nc.vector.tensor_scalar(place_i[:, 0:1], of, P - 1, None, ALU.bitwise_and).then_inc(s_place, 1)
                    nc.vector.tensor_scalar(place_i[:, 1:2], of, ROW_BITS + PLACE_BITS, None,
                                            ALU.logical_shift_right).then_inc(s_place, 1)
                    nc.vector.tensor_scalar(place_i[:, 2:3], of, ROW_BITS, PLACES - 1, ALU.logical_shift_right,
                                            ALU.bitwise_and).then_inc(s_place, 1)
                    dve.wait_ge(s_place, n * 5 + 3)
                    nc.vector.tensor_copy(place[:, :], place_i[:, :]).then_inc(s_place, 1)
                    dve.wait_ge(s_place, n * 5 + 4)
                    nc.vector.scalar_tensor_tensor(out=set_row[:, :], in0=place[:, 1:2], scalar=float(P),
                                                   in1=place[:, 0:1], op0=ALU.mult, op1=ALU.add).then_inc(s_place, 1)
                    for r in range(ROUNDS):
                        nc.vector.tensor_tensor(hot_place[r][:, :], iota[:, r * HB:r * HB + HB],
                                                place[:, 2:3].to_broadcast([P, HB]), ALU.is_equal).then_inc(s_hot, 1)
                    dve.wait_ge(s_place, n * 5 + 5)
                    nc.vector.tensor_tensor(
                        hot_row[:, :, :].rearrange("p c e -> p (c e)"), iota_sets[:, :, :].rearrange("p c e -> p (c e)"),
                        set_row[:, :].to_broadcast([P, SETS * P]), ALU.is_equal).then_inc(s_hot, 1)

                def pick(n, r):
                    dve.wait_ge(s_round, n * ROUNDS + r + 1)
                    rows = pick_ps[r][:, :].rearrange("p (k f) -> p k f", f=H)
                    hot = hot_place[r][:, :].unsqueeze(2).to_broadcast([P, HB, H])
                    if r == 0:
                        nc.vector.tensor_mul(kept[:, :, :], rows, hot).then_inc(s_picked, 1)
                    else:
                        dve.wait_ge(s_picked, n * ROUNDS + r)
                        dve.nop(nofuse=True)
                        nc.vector.copy_predicated(kept[:, :, :], hot, rows).then_inc(s_picked, 1)

                def place_rows(n, slot):
                    dve.wait_ge(s_picked, n * ROUNDS + ROUNDS)
                    nc.vector.tensor_reduce(edge_in[:, slot, PICKED, XS], kept[:, :, :].rearrange("p k f -> p f k"),
                                            AX.X, ALU.add).then_inc(s_row, 1)

                def groups(k, j=None):
                    for u in range(B):
                        p, h = MADE[u]
                        slot = (u - h) % S
                        ends = j is not None and h == BESIDE_GROUPS[p] - 1
                        copy_inputs(k * B + (u + 1))
                        if j is None:
                            split(k * B + u, (k * B + u) * SPLIT, SPLIT)
                        elif h == 0 and u:
                            place_rows(j * NPICK + p - 1, (u - BESIDE_GROUPS[p - 1]) % S)
                        add_bias(k * B + u)
                        prepare(k * B + (u + 2), (u + 2) % S, k * (16 * TURNS) + 16 * ((u + 2) // S + 1))
                        if j is not None and h == 0:
                            find_rows(j * NPICK + p, slot, k * (16 * TURNS) + 16 * ((u + S) // S + 1))
                        if ends:
                            for r in range(ROUNDS):
                                pick(j * NPICK + p, r)
                        add_messages(k * B + u)
                        if ends and u == B - 1:
                            place_rows(j * NPICK + p, slot)

                with dve.Fori(0, ITERS) as k:
                    groups(k)
                split(SPAN, SPAN * SPLIT, NT - SPAN * SPLIT)
                with dve.Fori(0, LOTS) as b:
                    with dve.Fori(0, ITERS) as i:
                        groups(b * ITERS + i + ITERS, b * ITERS + i)
                    with dve.If(late == 0):
                        inner_lot(b)
                for g in range(REST, NG):
                    copy_inputs(g)
                    add_bias(g - 1)
                    if g < FULL:
                        tail = g + 1 == FULL
                        prepare(g + 1, (g + 1) % S, 16 * ((g + 1) // S + 1 + tail))
                    add_messages(g - 1)
                add_bias(FULL)
                add_messages(FULL)
                dve.wait_ge(s_added, NG)
                nc.vector.memset(done_mark[:, :], 0.0).then_inc(s_sums, 1)
            with dve.Else():
                any_tiles = edge_in[:, ANY, :, :]

                def any_group(g, loaded, tiles):
                    if tiles < T:
                        dve.wait_ge(a_rel, FULL * (NT + 1))
                        nc.vector.memset(dst_rel[:, tiles:T], -1.0)
                    dve.wait_ge(a_load, loaded)
                    nc.vector.tensor_copy(dst_rel[:, 0:tiles], dst_i[:, 0, 0:tiles]).then_inc(a_rel, 1)
                    for ends in (SRC, DST):
                        dve.wait_ge(a_T, g * 2 + (ends + 1))
                        nc.vector.tensor_copy(in_T[:, 0, :], in_ps[0][:, :])
                        nc.vector.tensor_copy(in_T[:, 1, :], in_ps[1][:, :]).then_inc(a_Tc, 1)
                    dve.wait_ge(a_z2, g + 1)
                    bias_z2().then_inc(a_biased, 1)
                    with dve.Fori(0, NT) as k:
                        dve.wait_ge(a_rel, g * (NT + 1) + k + 1)
                        nc.vector.tensor_tensor(
                            any_tiles, iota[:, :].unsqueeze(1).to_broadcast([P, T, P]),
                            dst_rel[:, :].unsqueeze(2).to_broadcast([P, T, P]), ALU.is_equal).then_inc(a_oh, 1)
                        dve.wait_ge(a_oh, g * NT + k + 1)
                        nc.vector.tensor_scalar(dst_rel[:, :], dst_rel[:, :], float(-P), None,
                                                ALU.add).then_inc(a_rel, 1)
                        dve.wait_ge(a_agg, g * NT + k + 1)
                        sums = node_T[H:P, bass.ds(k * P, P)]
                        nc.vector.tensor_add(sums, sums, agg_ps[H:P, 0:P]).then_inc(a_added, 1)

                for s in range(S):
                    dve.wait_ge(s_xg[s], 16 * T)
                nc.vector.memset(edge_in[:, SRC:DST + 1, :, :], 0.0).then_inc(a_clear, 1)
                with dve.Fori(0, FULL) as g:
                    any_group(g, g * 48 + 48, T)
                any_group(FULL, FULL * 48 + 48, TT)
                dve.wait_ge(a_added, NG * NT)
                nc.vector.memset(done_mark[:, :], 0.0).then_inc(s_sums, 1)

            with dve.If(late == 1):
                with dve.Fori(0, LOTS) as b:
                    inner_lot(b)
            update_lot(LOTS, LAST_T, xs[:, LOTS * LT:NT, :])

        @block.tensor
        def _(pe):
            pe.wait_ge(s_ident, 2)
            pe.wait_ge(s_chk, 2)
            nc.tensor.matmul(z1_ps[:, 0:Q * P], ones[:, :], base_diag[:, :, :].rearrange("p q c -> p (q c)"),
                             start=True, stop=True).then_inc(s_base, 1)
            pe.wait_ge(s_chk, 6)
            nc.tensor.transpose(z2_ps[0:2, 0:P], outside[:, :], ident[:, :]).then_inc(s_out_T, 1)

            pe.wait_ge(s_x, 16 * 2)
            for n, (a, b) in enumerate(xT_banks):
                if n >= 2:
                    pe.wait_ge((s_xT_a, s_xT_v)[n % 2], n // 2)
                for j, k in enumerate(range(a, b)):
                    last = nc.tensor.transpose(in_ps[n % 2][0:H, j * P:(j + 1) * P], xs[:, k, :], ident[:, :])
                last.then_inc(s_xT_ps, 1)
            pe.wait_ge(s_xT_a, -(-len(xT_banks) // 2))
            pe.wait_ge(s_xT_v, len(xT_banks) // 2)
            pe.wait_ge(s_w, 16 * n_weights)
            pe.wait_ge(s_flag, 1)

            def transpose_tiles(s):
                for t in range(T):
                    last = nc.tensor.transpose(in_ps[t // HT][:, t % HT * P:(t % HT + 1) * P],
                                               edge_in[:, s, t, :], ident[:, :])
                return last

            def transpose_inputs(g, s, gathered):
                pe.wait_ge(s_xwin, g + 1)
                pe.wait_ge(s_oh, g + 1)
                pe.wait_ge(s_eac, g + 1)
                pe.wait_ge(s_xg[s], gathered)
                transpose_tiles(s).then_inc(s_in_T, 1)
                nc.tensor.matmul(agg_ps[OH, 0:H], xwin[:, :], w1b[:, :], start=True, stop=True).then_inc(s_bwin, 1)

            def first_layer(g):
                pe.wait_ge(s_bwc, g + 1)
                pe.wait_ge(s_in1c, g + 1)
                nc.tensor.matmul(z1_ps[0:H, :], w_in[:, :], in_T[:, 0, :], start=True, stop=True)
                nc.tensor.matmul(z1_ps[H:P, :], w_in[:, :], in_T[:, 1, :], start=True, stop=True).then_inc(s_z1, 1)

            def by_edges():
                for c in range(HT):
                    last = nc.tensor.matmul(z2_ps[:, c * P:(c + 1) * P], h_T[:, c * P:(c + 1) * P], w2_bd[:, :],
                                            start=True, stop=True)
                return last

            def second_layer(g):
                pe.wait_ge(s_h, g + 1)
                by_edges().then_inc(s_z2, 1)

            def sum_by_node(s, nodes):
                for t in range(T):
                    last = nc.tensor.matmul(agg_ps[H:P, nodes], msg[:, t % HT, t // HT, :], edge_in[:, s, t, nodes],
                                            start=(t == 0), stop=(t == T - 1))
                return last

            def sum_messages(g, s):
                pe.wait_ge(s_msg, g + 1)
                sum_by_node(s, OH).then_inc(s_agg, 1)

            def update_lot(b, m, lot):
                half = m * P // 2
                for a in range(2):
                    last = nc.tensor.matmul(z2_ps[a * H:(a + 1) * H, 0:half], w3[:, :], lot[:, a * half:(a + 1) * half],
                                            start=True, stop=True)
                last.then_inc(s_z3, 1)
                pe.wait_ge(s_upd, b + 1)
                for c in range(m // 2):
                    last = nc.tensor.transpose(upd_ps[:, c * P:(c + 1) * P], upd_T[:, c * P:(c + 1) * P], ident[:, :])
                last.then_inc(s_updT, 1)

            def inner_lot(b):
                pe.wait_ge(s_lot, b + 1)
                update_lot(b, LT, lot_T)

            general = pe.value_load(flags_i[0:1, 0:1], min_val=0, max_val=1)
            late = pe.value_load(flags_i[1:2, 0:1], min_val=0, max_val=1)
            with pe.If(general == 0):
                transpose_inputs(0, 0, 16 * T)
                first_layer(0)
                def picked_tiles(s, turn):
                    by_turn = [s in slots for slots in PICKED_SLOTS]
                    return sum(by_turn), sum(by_turn[:turn])

                def transpose_hot_row(n):
                    pe.wait_ge(s_hot, n * 3 + 3)
                    for c in range(SETS):
                        last = nc.tensor.transpose(pick_ps[c // HT][:, c % HT * P:(c % HT + 1) * P], hot_row[:, c, :],
                                                   ident[:, :])
                    last.then_inc(s_hotT, 1)

                def pick_piece(n, piece):
                    r, c = PIECES[piece]
                    a = c * PLACES + r * HB
                    b = min(NT, a + HB)
                    if piece == 0:
                        pe.wait_ge(s_rowsT, n * 2 + 2)
                    done = (r, c + 1) not in PIECES
                    for i in range(PARTS):
                        last = nc.tensor.matmul(pick_ps[r][:, 0:(b - a) * H], rows_T[:, c, :],
                                                parts[:, i, a:b, :].rearrange("p k f -> p (k f)"),
                                                start=(c == 0 and i == 0), stop=(done and i == PARTS - 1))
                    if done:
                        last.then_inc(s_round, 1)

                def groups(k, j=None):
                    for u in range(B):
                        g, s, turn = k * B + (u + 1), (u + 1) % S, (u + 1) // S
                        p, h = MADE[u]
                        beside = BESIDE[BESIDE_GROUPS[p]]
                        ahead = [sum(sum(n) for n in beside[:h])]

                        def pieces(place):
                            if j is not None:
                                for _ in range(beside[h][place]):
                                    pick_piece(j * NPICK + p, ahead[0])
                                    ahead[0] += 1

                        gathered = k * (16 * T * TURNS) + 16 * T * (turn + 1)
                        if j is not None:
                            each, now = picked_tiles(s, turn)
                            gathered = j * (16 * (T * TURNS - each)) + 16 * (T * (FIRST + turn) - now)
                            for p_done in range(NPICK):
                                if PICKED_AT[p_done] + S == u + 1:
                                    pe.wait_ge(s_row, j * NPICK + p_done + 1)
                        transpose_inputs(g, s, gathered)
                        if j is not None and h == 1:
                            transpose_hot_row(j * NPICK + p)
                        pieces(AFTER_INPUTS)
                        second_layer(k * B + u)
                        pieces(AFTER_SECOND)
                        first_layer(g)
                        pieces(AFTER_FIRST)
                        sum_messages(k * B + u, u % S)
                        pieces(AFTER_SUMS)

                with pe.Fori(0, ITERS) as k:
                    groups(k)
                with pe.Fori(0, LOTS) as b:
                    with pe.Fori(0, ITERS) as i:
                        groups(b * ITERS + i + ITERS, b * ITERS + i)
                    with pe.If(late == 0):
                        inner_lot(b)
                for g in range(REST, NG):
                    each, _ = picked_tiles(g % S, 0)
                    gathered = T * (g // S) + (TT if g == FULL else T) - each * (BODIES - ITERS)
                    if each:
                        pe.wait_ge(s_row, NPICK * (BODIES - ITERS))
                    transpose_inputs(g, g % S, 16 * gathered)
                    second_layer(g - 1)
                    first_layer(g)
                    sum_messages(g - 1, (g - 1) % S)
                second_layer(FULL)
                sum_messages(FULL, FULL % S)
            with pe.Else():
                def any_group(g, gathered):
                    pe.wait_ge(a_eac, g + 1)
                    for ends, w in ((SRC, w_in), (DST, w_dst)):
                        pe.wait_ge(a_gath[ends], gathered)
                        transpose_tiles(ends).then_inc(a_T, 1)
                        pe.wait_ge(a_Tc, g * 2 + (ends + 1))
                        for half in range(2):
                            last = nc.tensor.matmul(z1_ps[half * H:(half + 1) * H, :], w[:, :], in_T[:, half, :],
                                                    start=(ends == SRC), stop=(ends == DST))
                    last.then_inc(a_z1, 1)
                    pe.wait_ge(a_h, g + 1)
                    by_edges().then_inc(a_z2, 1)
                    pe.wait_ge(a_msg, g + 1)
                    pe.nop(nofuse=True)
                    with pe.Fori(0, NT) as k:
                        pe.wait_ge(a_oh, g * NT + k + 1)
                        sum_by_node(ANY, slice(0, P)).then_inc(a_agg, 1)

                with pe.Fori(0, FULL) as g:
                    any_group(g, g * (16 * T) + 16 * T)
                any_group(FULL, 16 * (T * FULL + TT))

            with pe.If(late == 1):
                with pe.Fori(0, LOTS) as b:
                    inner_lot(b)
            pe.wait_ge(s_sums, 1)
            pe.wait_ge(s_res, LOTS)
            update_lot(LOTS, LAST_T, node_T[:, LOTS * LN:NPAD])


_INS = ["x", "src", "dst", "edge_attr_16", "L0_gnn_W1", "L0_gnn_b1", "L0_gnn_W2", "L0_gnn_b2", "L0_gnn_W3", "L0_gnn_b3"]


def kernel(**inputs):
    import numpy as _np
    import concourse.bacc as _bacc
    from concourse import mybir as _mybir
    from concourse.bass_utils import run_bass_kernel_spmd as _run

    nc = _bacc.Bacc("TRN2", target_bir_lowering=False, num_devices=1)
    arrays, args = {}, []
    for name in _INS:
        a = _np.ascontiguousarray(inputs[name])
        arrays[f"in_{name}_dram"] = a
        args.append(nc.dram_tensor(f"in_{name}_dram", a.shape, _mybir.dt.from_np(a.dtype), kind="ExternalInput").ap())
    out = nc.dram_tensor("out_0_dram", inputs["x"].shape, _mybir.dt.float32, kind="ExternalOutput").ap()
    gnn_layer(nc, *args, out)
    r = _run(nc, [arrays], core_ids=[0])
    return r.results[0]["out_0_dram"]
```
